# Optimizing a Trainium2 kernel written in Bass

```python
import numpy as np
import jax
import jax.numpy as jnp

def _softmax(x, axis=-1):
    return jax.nn.softmax(x, axis=axis)

def _gelu(x):
    return jax.nn.gelu(x, approximate=True)

def _silu(x):
    return jax.nn.silu(x)

def _sigmoid(x):
    return jax.nn.sigmoid(x)

def _layernorm(x, axis=-1, eps=1e-05):
    m = jnp.mean(x, axis=axis, keepdims=True)
    v = jnp.var(x, axis=axis, keepdims=True)
    return (x - m) / jnp.sqrt(v + eps)

def _scatter_add(tgt, idx, src, axis=0):
    return tgt.at[idx].add(src)

def _segment_sum(src, seg, n):
    return jax.ops.segment_sum(src, seg, n)
kernel_name = 'mk_hybrid_d2_jaxref_r4_a3e6c0'

def setup_inputs(seed: int=0):
    np.random.seed(seed)
    _w = jnp.asarray

    def _L0_attn_a_setup():
        import jax, jax.numpy as jnp
        import numpy as np
        from jax.scipy.linalg import solve_triangular
        B, T, D = (2, 1024, 256)
        HEAD_DIM = 128
        CHUNK = 64

        def _forward(out, W_write, W_read, W_alpha, W_beta, A_log, dt_bias):
            Bs, Ts, Ds = out.shape
            d, C = (HEAD_DIM, CHUNK)
            H = Ds // d
            x = out.astype(jnp.float32)
            rk = x.reshape(Bs, Ts, H, d)
            rk = rk / jnp.maximum(jnp.linalg.norm(rk, axis=-1, keepdims=True), 1e-12)
            rk = jnp.swapaxes(rk, 1, 2)
            wk = jnp.pad(rk[:, :, :-1], ((0, 0), (0, 0), (1, 0), (0, 0)))
            v = jnp.einsum('btd,ed->bte', x, W_write).reshape(Bs, Ts, H, d)
            v = jnp.swapaxes(v, 1, 2)
            beta = jax.nn.sigmoid(jnp.einsum('btd,hd->bth', x, W_beta))
            beta = jnp.swapaxes(beta, 1, 2)[..., None]
            log_decay = -jnp.exp(A_log)[None, None, :] * jax.nn.softplus(jnp.einsum('btd,hd->bth', x, W_alpha) + dt_bias)
            log_decay = jnp.swapaxes(log_decay, 1, 2)
            v_scaled = v * beta
            wk_scaled = wk * beta
            pad = -Ts % C
            if pad:
                p4 = ((0, 0), (0, 0), (0, pad), (0, 0))
                rk = jnp.pad(rk, p4)
                wk = jnp.pad(wk, p4)
                v_scaled = jnp.pad(v_scaled, p4)
                wk_scaled = jnp.pad(wk_scaled, p4)
                log_decay = jnp.pad(log_decay, ((0, 0), (0, 0), (0, pad)))
            Tp = Ts + pad
            N = Tp // C
            chunk = lambda a: a.reshape(Bs, H, N, C, d)
            rk, wk, v_scaled, wk_scaled = map(chunk, (rk, wk, v_scaled, wk_scaled))
            log_decay = log_decay.reshape(Bs, H, N, C)
            cum = jnp.cumsum(log_decay, -1)
            L_mask = jnp.tril(jnp.exp(jnp.tril(cum[..., :, None] - cum[..., None, :])))
            decay_exp = jnp.exp(cum)[..., None]
            chunk_end_decay = jnp.exp(cum[..., -1])
            M = jnp.tril(-(wk_scaled @ jnp.swapaxes(wk, -1, -2)) * L_mask, -1)
            eye = jnp.eye(C, dtype=x.dtype)
            A = solve_triangular(eye - M, jnp.broadcast_to(eye, M.shape), lower=True, unit_diagonal=True)
            intra = jnp.tril(rk @ jnp.swapaxes(wk, -1, -2) * L_mask, -1)
            rk_decay = rk * decay_exp
            tail_decay = jnp.exp(cum[..., -1:] - cum)[..., None]
            wk_pos = jnp.swapaxes(wk * tail_decay, -1, -2)
            wk_scaled_dec = wk_scaled * decay_exp
            toN = lambda a: jnp.moveaxis(a, 2, 0)

            def step(S, inp):
                A_i, vsc_i, wkd_i, rkd_i, intra_i, wkp_i, ced_i = inp
                v_new = A_i @ vsc_i - A_i @ wkd_i @ S
                o_i = rkd_i @ S + intra_i @ v_new
                S = ced_i[..., None, None] * S + wkp_i @ v_new
                return (S, o_i)
            S0 = jnp.zeros((Bs, H, d, d), x.dtype)
            _, o = jax.lax.scan(step, S0, (toN(A), toN(v_scaled), toN(wk_scaled_dec), toN(rk_decay), toN(intra), toN(wk_pos), jnp.moveaxis(chunk_end_decay, 2, 0)))
            o = jnp.moveaxis(o, 0, 2).reshape(Bs, H, Tp, d)
            o = jnp.swapaxes(o, 1, 2).reshape(Bs, Tp, Ds)[:, :Ts]
            return out + jnp.einsum('btd,ed->bte', o, W_read).astype(out.dtype)
        key = jax.random.key(seed)
        ks = jax.random.split(key, 7)
        H = D // HEAD_DIM
        out = jax.random.normal(ks[0], (B, T, D), dtype=jnp.float32)
        scale = D ** (-0.5)
        W_write = jax.random.normal(ks[1], (D, D), jnp.float32) * scale
        W_read = jax.random.normal(ks[2], (D, D), jnp.float32) * scale
        W_alpha = jax.random.normal(ks[3], (H, D), jnp.float32) * scale
        W_beta = jax.random.normal(ks[4], (H, D), jnp.float32) * scale
        A_log = jnp.log(jax.random.uniform(ks[5], (H,), jnp.float32, 0.05, 16.0))
        dt_bias = jnp.ones((H,), jnp.float32)
        return {'out': out, 'W_write': W_write, 'W_read': W_read, 'W_alpha': W_alpha, 'W_beta': W_beta, 'A_log': A_log, 'dt_bias': dt_bias}
    _L0_attn_a_in = _L0_attn_a_setup()

    def _L0_attn_b_setup():
        import jax, jax.numpy as jnp
        import numpy as np
        import math
        B, N, D = (2, 512, 256)
        H = 16
        DH = D // H
        CG_ITERS = 30
        THRESHOLD = 0.99
        LAMBDA_INIT = 1.0
        LAMBDA_LOWER = 0.25
        NORM_EPS = 1e-05

        def l2norm(x, eps=1e-06):
            return x * jax.lax.rsqrt(jnp.sum(x * x, axis=-1, keepdims=True) + eps)

        def cg_solve(A, rhs, n_iters):
            x0 = jnp.zeros_like(rhs)
            rs0 = jnp.sum(rhs * rhs, axis=-1)

            def step(carry, _):
                x, r, p, rs = carry
                Ap = jnp.einsum('bhij,bhj->bhi', A, p)
                alpha = rs / (jnp.sum(p * Ap, axis=-1) + 1e-12)
                x = x + alpha[..., None] * p
                r = r - alpha[..., None] * Ap
                rs_new = jnp.sum(r * r, axis=-1)
                p = r + (rs_new / (rs + 1e-12))[..., None] * p
                return ((x, r, p, rs_new), None)
            (x, _, _, _), _ = jax.lax.scan(step, (x0, rhs, rhs, rs0), None, length=n_iters)
            return x
        key = jax.random.key(seed)
        ks = jax.random.split(key, 10)
        std = 0.02
        inp = {'x': jax.random.normal(ks[0], (B, N, D), dtype=jnp.float32), 'Wq': jax.random.normal(ks[1], (D, D), dtype=jnp.float32) * std, 'Wk': jax.random.normal(ks[2], (D, D), dtype=jnp.float32) * std, 'Wv': jax.random.normal(ks[3], (D, D), dtype=jnp.float32) * std, 'Wf': jax.random.normal(ks[4], (D, H), dtype=jnp.float32) * std, 'Wbet': jax.random.normal(ks[5], (D, H), dtype=jnp.float32) * std, 'Wo': jax.random.normal(ks[6], (D, D), dtype=jnp.float32) * std, 'delta': jnp.full((H,), math.log(THRESHOLD / (1.0 - THRESHOLD)), dtype=jnp.float32), 'lamb_params': jnp.full((D,), math.log(math.exp(math.exp(LAMBDA_INIT - LAMBDA_LOWER)) - 1.0), dtype=jnp.float32), 'norm_weight': jnp.ones((D,), dtype=jnp.float32), 'gate_w1': jax.random.normal(ks[7], (D, DH), dtype=jnp.float32) * std, 'gate_w2': jax.random.normal(ks[8], (DH, D), dtype=jnp.float32) * std}
        return inp
    _L0_attn_b_in = _L0_attn_b_setup()

    def _L0_ffn_setup():
        import jax, jax.numpy as jnp
        import numpy as np
        D = 256
        H = 16
        HD = D // H
        L = 64
        E = 8
        B, T = (4, 512)
        EPS = 1e-06

        def _glorot(k, shape):
            fan_in, fan_out = (shape[-2], shape[-1])
            lim = np.sqrt(6.0 / (fan_in + fan_out)).astype(np.float32)
            return jax.random.uniform(k, shape, jnp.float32, -lim, lim)

        def _rmsnorm(x, gamma):
            return gamma * x * jax.lax.rsqrt(jnp.mean(x * x, axis=-1, keepdims=True) + EPS)
        key = jax.random.key(seed)
        ks = jax.random.split(key, 8)
        return {'x': jax.random.normal(ks[0], (B, T, D), jnp.float32), 'gamma1': jnp.ones((D,), jnp.float32), 'Wq': _glorot(ks[1], (D, D)), 'bq': jnp.zeros((D,), jnp.float32), 'Wdown': _glorot(ks[2], (D, L)), 'bdown': jnp.zeros((L,), jnp.float32), 'Wup': _glorot(ks[3], (L, 2 * D)), 'bup': jnp.zeros((2 * D,), jnp.float32), 'Wo': _glorot(ks[4], (D, D)), 'bo': jnp.zeros((D,), jnp.float32), 'gamma2': jnp.ones((D,), jnp.float32), 'Wg': _glorot(ks[5], (D, E)), 'bg': jnp.zeros((E,), jnp.float32), 'We': _glorot(ks[6], (E, D, D))}
    _L0_ffn_in = _L0_ffn_setup()

    def _L1_attn_a_setup():
        import jax, jax.numpy as jnp
        import numpy as np
        N_HEADS = 16
        WINDOW = 64

        def _sliding_window_bias(seq_len: int) -> jnp.ndarray:
            i = jnp.arange(seq_len)[:, None]
            j = jnp.arange(seq_len)[None, :]
            allowed = jnp.abs(i - j) <= WINDOW
            return jnp.where(allowed, 0.0, -jnp.inf).astype(jnp.float32)
        key = jax.random.key(seed)
        ks = jax.random.split(key, 6)
        B, S, D = (2, 512, 256)
        std = 0.02
        x = jax.random.normal(ks[0], (B, S, D), dtype=jnp.float32)
        wq = jax.random.normal(ks[1], (D, D), dtype=jnp.float32) * std
        wk = jax.random.normal(ks[2], (D, D), dtype=jnp.float32) * std
        wv = jax.random.normal(ks[3], (D, D), dtype=jnp.float32) * std
        wo = jax.random.normal(ks[4], (D, D), dtype=jnp.float32) * std
        bq = jnp.zeros((D,), jnp.float32)
        bk = jnp.zeros((D,), jnp.float32)
        bv = jnp.zeros((D,), jnp.float32)
        bo = jnp.zeros((D,), jnp.float32)
        return {'x': x, 'wq': wq, 'bq': bq, 'wk': wk, 'bk': bk, 'wv': wv, 'bv': bv, 'wo': wo, 'bo': bo}
    _L1_attn_a_in = _L1_attn_a_setup()

    def _L1_attn_b_setup():
        import jax, jax.numpy as jnp
        import numpy as np
        HIDDEN = 256
        NUM_HEADS = 16
        NUM_KV = 4
        HEAD_DIM = HIDDEN // NUM_HEADS
        GROUPS = NUM_HEADS // NUM_KV
        SCALE = HEAD_DIM ** 0.5
        key = jax.random.key(seed)
        ks = jax.random.split(key, 9)
        s = 0.02
        B, N = (4, 512)
        return {'x': jax.random.normal(ks[0], (B, N, HIDDEN), dtype=jnp.float32), 'Wq': jax.random.normal(ks[1], (HIDDEN, NUM_HEADS * HEAD_DIM), dtype=jnp.float32) * s, 'bq': jnp.zeros((NUM_HEADS * HEAD_DIM,), dtype=jnp.float32), 'Wk': jax.random.normal(ks[2], (HIDDEN, NUM_KV * HEAD_DIM), dtype=jnp.float32) * s, 'bk': jnp.zeros((NUM_KV * HEAD_DIM,), dtype=jnp.float32), 'Wv': jax.random.normal(ks[3], (HIDDEN, NUM_KV * HEAD_DIM), dtype=jnp.float32) * s, 'bv': jnp.zeros((NUM_KV * HEAD_DIM,), dtype=jnp.float32), 'Wo': jax.random.normal(ks[4], (NUM_HEADS * HEAD_DIM, HIDDEN), dtype=jnp.float32) * s, 'bo': jnp.zeros((HIDDEN,), dtype=jnp.float32)}
    _L1_attn_b_in = _L1_attn_b_setup()

    def _L1_ffn_setup():
        import jax, jax.numpy as jnp
        import numpy as np
        D_MODEL = 256
        key = jax.random.key(seed)
        k_x, k_w, k_a1, k_a2 = jax.random.split(key, 4)
        x = jax.random.normal(k_x, (4, 512, D_MODEL), dtype=jnp.float32)
        weight = jax.random.normal(k_w, (D_MODEL, D_MODEL), dtype=jnp.float32) * 0.02
        aux_weight1 = jax.random.normal(k_a1, (D_MODEL, D_MODEL), dtype=jnp.float32) * 0.02
        aux_weight2 = jax.random.normal(k_a2, (D_MODEL, D_MODEL), dtype=jnp.float32) * 0.02
        bias = jnp.zeros((D_MODEL,), dtype=jnp.float32)
        return {'x': x, 'weight': weight, 'aux_weight1': aux_weight1, 'aux_weight2': aux_weight2, 'bias': bias}
    _L1_ffn_in = _L1_ffn_setup()
    _d = {'L0_attn_a_out': _L0_attn_a_in['out'], 'L0_attn_a_W_write': _L0_attn_a_in['W_write'], 'L0_attn_a_W_read': _L0_attn_a_in['W_read'], 'L0_attn_a_W_alpha': _L0_attn_a_in['W_alpha'], 'L0_attn_a_W_beta': _L0_attn_a_in['W_beta'], 'L0_attn_a_A_log': _L0_attn_a_in['A_log'], 'L0_attn_a_dt_bias': _L0_attn_a_in['dt_bias'], 'L0_attn_b_Wq': _L0_attn_b_in['Wq'], 'L0_attn_b_Wk': _L0_attn_b_in['Wk'], 'L0_attn_b_Wv': _L0_attn_b_in['Wv'], 'L0_attn_b_Wf': _L0_attn_b_in['Wf'], 'L0_attn_b_Wbet': _L0_attn_b_in['Wbet'], 'L0_attn_b_Wo': _L0_attn_b_in['Wo'], 'L0_attn_b_delta': _L0_attn_b_in['delta'], 'L0_attn_b_lamb_params': _L0_attn_b_in['lamb_params'], 'L0_attn_b_norm_weight': _L0_attn_b_in['norm_weight'], 'L0_attn_b_gate_w1': _L0_attn_b_in['gate_w1'], 'L0_attn_b_gate_w2': _L0_attn_b_in['gate_w2'], 'L0_ffn_gamma1': _L0_ffn_in['gamma1'], 'L0_ffn_Wq': _L0_ffn_in['Wq'], 'L0_ffn_bq': _L0_ffn_in['bq'], 'L0_ffn_Wdown': _L0_ffn_in['Wdown'], 'L0_ffn_bdown': _L0_ffn_in['bdown'], 'L0_ffn_Wup': _L0_ffn_in['Wup'], 'L0_ffn_bup': _L0_ffn_in['bup'], 'L0_ffn_Wo': _L0_ffn_in['Wo'], 'L0_ffn_bo': _L0_ffn_in['bo'], 'L0_ffn_gamma2': _L0_ffn_in['gamma2'], 'L0_ffn_Wg': _L0_ffn_in['Wg'], 'L0_ffn_bg': _L0_ffn_in['bg'], 'L0_ffn_We': _L0_ffn_in['We'], 'L1_attn_a_wq': _L1_attn_a_in['wq'], 'L1_attn_a_bq': _L1_attn_a_in['bq'], 'L1_attn_a_wk': _L1_attn_a_in['wk'], 'L1_attn_a_bk': _L1_attn_a_in['bk'], 'L1_attn_a_wv': _L1_attn_a_in['wv'], 'L1_attn_a_bv': _L1_attn_a_in['bv'], 'L1_attn_a_wo': _L1_attn_a_in['wo'], 'L1_attn_a_bo': _L1_attn_a_in['bo'], 'L1_attn_b_Wq': _L1_attn_b_in['Wq'], 'L1_attn_b_bq': _L1_attn_b_in['bq'], 'L1_attn_b_Wk': _L1_attn_b_in['Wk'], 'L1_attn_b_bk': _L1_attn_b_in['bk'], 'L1_attn_b_Wv': _L1_attn_b_in['Wv'], 'L1_attn_b_bv': _L1_attn_b_in['bv'], 'L1_attn_b_Wo': _L1_attn_b_in['Wo'], 'L1_attn_b_bo': _L1_attn_b_in['bo'], 'L1_ffn_weight': _L1_ffn_in['weight'], 'L1_ffn_aux_weight1': _L1_ffn_in['aux_weight1'], 'L1_ffn_aux_weight2': _L1_ffn_in['aux_weight2'], 'L1_ffn_bias': _L1_ffn_in['bias']}
    _x0 = _d['L0_attn_a_out']
    _d['L0_attn_a_out'] = jax.random.normal(jax.random.fold_in(jax.random.key(seed), 1), (8, 1024, 256), dtype=_x0.dtype)
    del _x0
    return _d

def reference(L0_attn_a_out, L0_attn_a_W_write, L0_attn_a_W_read, L0_attn_a_W_alpha, L0_attn_a_W_beta, L0_attn_a_A_log, L0_attn_a_dt_bias, L0_attn_b_Wq, L0_attn_b_Wk, L0_attn_b_Wv, L0_attn_b_Wf, L0_attn_b_Wbet, L0_attn_b_Wo, L0_attn_b_delta, L0_attn_b_lamb_params, L0_attn_b_norm_weight, L0_attn_b_gate_w1, L0_attn_b_gate_w2, L0_ffn_gamma1, L0_ffn_Wq, L0_ffn_bq, L0_ffn_Wdown, L0_ffn_bdown, L0_ffn_Wup, L0_ffn_bup, L0_ffn_Wo, L0_ffn_bo, L0_ffn_gamma2, L0_ffn_Wg, L0_ffn_bg, L0_ffn_We, L1_attn_a_wq, L1_attn_a_bq, L1_attn_a_wk, L1_attn_a_bk, L1_attn_a_wv, L1_attn_a_bv, L1_attn_a_wo, L1_attn_a_bo, L1_attn_b_Wq, L1_attn_b_bq, L1_attn_b_Wk, L1_attn_b_bk, L1_attn_b_Wv, L1_attn_b_bv, L1_attn_b_Wo, L1_attn_b_bo, L1_ffn_weight, L1_ffn_aux_weight1, L1_ffn_aux_weight2, L1_ffn_bias):

    def _L0_attn_a_ref(out, W_write, W_read, W_alpha, W_beta, A_log, dt_bias):
        import jax, jax.numpy as jnp
        import numpy as np
        from jax.scipy.linalg import solve_triangular
        B, T, D = (2, 1024, 256)
        HEAD_DIM = 128
        CHUNK = 64

        def _forward(out, W_write, W_read, W_alpha, W_beta, A_log, dt_bias):
            Bs, Ts, Ds = out.shape
            d, C = (HEAD_DIM, CHUNK)
            H = Ds // d
            x = out.astype(jnp.float32)
            rk = x.reshape(Bs, Ts, H, d)
            rk = rk / jnp.maximum(jnp.linalg.norm(rk, axis=-1, keepdims=True), 1e-12)
            rk = jnp.swapaxes(rk, 1, 2)
            wk = jnp.pad(rk[:, :, :-1], ((0, 0), (0, 0), (1, 0), (0, 0)))
            v = jnp.einsum('btd,ed->bte', x, W_write).reshape(Bs, Ts, H, d)
            v = jnp.swapaxes(v, 1, 2)
            beta = jax.nn.sigmoid(jnp.einsum('btd,hd->bth', x, W_beta))
            beta = jnp.swapaxes(beta, 1, 2)[..., None]
            log_decay = -jnp.exp(A_log)[None, None, :] * jax.nn.softplus(jnp.einsum('btd,hd->bth', x, W_alpha) + dt_bias)
            log_decay = jnp.swapaxes(log_decay, 1, 2)
            v_scaled = v * beta
            wk_scaled = wk * beta
            pad = -Ts % C
            if pad:
                p4 = ((0, 0), (0, 0), (0, pad), (0, 0))
                rk = jnp.pad(rk, p4)
                wk = jnp.pad(wk, p4)
                v_scaled = jnp.pad(v_scaled, p4)
                wk_scaled = jnp.pad(wk_scaled, p4)
                log_decay = jnp.pad(log_decay, ((0, 0), (0, 0), (0, pad)))
            Tp = Ts + pad
            N = Tp // C
            chunk = lambda a: a.reshape(Bs, H, N, C, d)
            rk, wk, v_scaled, wk_scaled = map(chunk, (rk, wk, v_scaled, wk_scaled))
            log_decay = log_decay.reshape(Bs, H, N, C)
            cum = jnp.cumsum(log_decay, -1)
            L_mask = jnp.tril(jnp.exp(jnp.tril(cum[..., :, None] - cum[..., None, :])))
            decay_exp = jnp.exp(cum)[..., None]
            chunk_end_decay = jnp.exp(cum[..., -1])
            M = jnp.tril(-(wk_scaled @ jnp.swapaxes(wk, -1, -2)) * L_mask, -1)
            eye = jnp.eye(C, dtype=x.dtype)
            A = solve_triangular(eye - M, jnp.broadcast_to(eye, M.shape), lower=True, unit_diagonal=True)
            intra = jnp.tril(rk @ jnp.swapaxes(wk, -1, -2) * L_mask, -1)
            rk_decay = rk * decay_exp
            tail_decay = jnp.exp(cum[..., -1:] - cum)[..., None]
            wk_pos = jnp.swapaxes(wk * tail_decay, -1, -2)
            wk_scaled_dec = wk_scaled * decay_exp
            toN = lambda a: jnp.moveaxis(a, 2, 0)

            def step(S, inp):
                A_i, vsc_i, wkd_i, rkd_i, intra_i, wkp_i, ced_i = inp
                v_new = A_i @ vsc_i - A_i @ wkd_i @ S
                o_i = rkd_i @ S + intra_i @ v_new
                S = ced_i[..., None, None] * S + wkp_i @ v_new
                return (S, o_i)
            S0 = jnp.zeros((Bs, H, d, d), x.dtype)
            _, o = jax.lax.scan(step, S0, (toN(A), toN(v_scaled), toN(wk_scaled_dec), toN(rk_decay), toN(intra), toN(wk_pos), jnp.moveaxis(chunk_end_decay, 2, 0)))
            o = jnp.moveaxis(o, 0, 2).reshape(Bs, H, Tp, d)
            o = jnp.swapaxes(o, 1, 2).reshape(Bs, Tp, Ds)[:, :Ts]
            return out + jnp.einsum('btd,ed->bte', o, W_read).astype(out.dtype)
        return _forward(out, W_write, W_read, W_alpha, W_beta, A_log, dt_bias)

    def _L0_attn_b_ref(x, Wq, Wk, Wv, Wf, Wbet, Wo, delta, lamb_params, norm_weight, gate_w1, gate_w2):
        import jax, jax.numpy as jnp
        import numpy as np
        import math
        B, N, D = (2, 512, 256)
        H = 16
        DH = D // H
        CG_ITERS = 30
        THRESHOLD = 0.99
        LAMBDA_INIT = 1.0
        LAMBDA_LOWER = 0.25
        NORM_EPS = 1e-05

        def l2norm(x, eps=1e-06):
            return x * jax.lax.rsqrt(jnp.sum(x * x, axis=-1, keepdims=True) + eps)

        def cg_solve(A, rhs, n_iters):
            x0 = jnp.zeros_like(rhs)
            rs0 = jnp.sum(rhs * rhs, axis=-1)

            def step(carry, _):
                x, r, p, rs = carry
                Ap = jnp.einsum('bhij,bhj->bhi', A, p)
                alpha = rs / (jnp.sum(p * Ap, axis=-1) + 1e-12)
                x = x + alpha[..., None] * p
                r = r - alpha[..., None] * Ap
                rs_new = jnp.sum(r * r, axis=-1)
                p = r + (rs_new / (rs + 1e-12))[..., None] * p
                return ((x, r, p, rs_new), None)
            (x, _, _, _), _ = jax.lax.scan(step, (x0, rhs, rhs, rs0), None, length=n_iters)
            return x
        b, n, d = x.shape
        h, dh = (H, DH)
        q = (x @ Wq).reshape(b, n, h, dh)
        k = (x @ Wk).reshape(b, n, h, dh)
        v = (x @ Wv).reshape(b, n, h, dh)
        log_f = jax.nn.log_sigmoid(x @ Wf + delta)
        beta = jax.nn.sigmoid(x @ Wbet)
        lamb = (jax.nn.softplus(lamb_params) + LAMBDA_LOWER).reshape(h, dh)
        q = l2norm(q)
        k = l2norm(k)
        diag_lamb = lamb[:, :, None] * jnp.eye(dh, dtype=x.dtype)
        qT = q.transpose(1, 0, 2, 3)
        kT = k.transpose(1, 0, 2, 3)
        vT = v.transpose(1, 0, 2, 3)
        fT = log_f.transpose(1, 0, 2)
        bT = beta.transpose(1, 0, 2)

        def step(carry, inp):
            h_kk, h_kv = carry
            qt, kt, vt, ft, bt = inp
            fexp = jnp.exp(ft)[..., None, None]
            bkt = bt[..., None] * kt
            h_kk = fexp * h_kk + jnp.einsum('bhi,bhj->bhij', bkt, kt)
            h_kv = fexp * h_kv + jnp.einsum('bhi,bhj->bhij', bkt, vt)
            A = h_kk + diag_lamb
            qs = cg_solve(A, qt, CG_ITERS)
            ot = jnp.einsum('bhi,bhij->bhj', qs, h_kv)
            return ((h_kk, h_kv), ot)
        init = (jnp.zeros((b, h, dh, dh), dtype=x.dtype), jnp.zeros((b, h, dh, dh), dtype=x.dtype))
        _, oT = jax.lax.scan(step, init, (qT, kT, vT, fT, bT))
        o = oT.transpose(1, 0, 2, 3)
        gate = jax.nn.sigmoid(x @ gate_w1 @ gate_w2).reshape(b, n, h, dh)
        og = o * gate
        og = og * jax.lax.rsqrt(jnp.mean(og * og, axis=-1, keepdims=True) + NORM_EPS)
        out = og.reshape(b, n, d) * norm_weight
        return out @ Wo

    def _L0_ffn_ref(x, gamma1, Wq, bq, Wdown, bdown, Wup, bup, Wo, bo, gamma2, Wg, bg, We):
        import jax, jax.numpy as jnp
        import numpy as np
        D = 256
        H = 16
        HD = D // H
        L = 64
        E = 8
        B, T = (4, 512)
        EPS = 1e-06

        def _glorot(k, shape):
            fan_in, fan_out = (shape[-2], shape[-1])
            lim = np.sqrt(6.0 / (fan_in + fan_out)).astype(np.float32)
            return jax.random.uniform(k, shape, jnp.float32, -lim, lim)

        def _rmsnorm(x, gamma):
            return gamma * x * jax.lax.rsqrt(jnp.mean(x * x, axis=-1, keepdims=True) + EPS)
        b, t = (x.shape[0], x.shape[1])
        h = _rmsnorm(x, gamma1)
        q = (h @ Wq + bq).reshape(b, t, H, HD)
        kv = ((h @ Wdown + bdown) @ Wup + bup).reshape(b, t, H, 2 * HD)
        k, v = jnp.split(kv, 2, axis=-1)
        att = jnp.einsum('bthd,btgd->bthg', q, k) / np.sqrt(HD).astype(np.float32)
        att = jax.nn.softmax(att, axis=-1)
        out = jnp.einsum('bthg,btgd->bthd', att, v).reshape(b, t, D)
        x = x + (out @ Wo + bo)
        h2 = _rmsnorm(x, gamma2)
        gate = jax.nn.softmax(h2 @ Wg + bg, axis=-1)
        combined = jnp.einsum('btd,edf,bte->btf', h2, We, gate)
        return x + combined

    def _L1_attn_a_ref(x, wq, bq, wk, bk, wv, bv, wo, bo):
        import jax, jax.numpy as jnp
        import numpy as np
        N_HEADS = 16
        WINDOW = 64

        def _sliding_window_bias(seq_len: int) -> jnp.ndarray:
            i = jnp.arange(seq_len)[:, None]
            j = jnp.arange(seq_len)[None, :]
            allowed = jnp.abs(i - j) <= WINDOW
            return jnp.where(allowed, 0.0, -jnp.inf).astype(jnp.float32)
        B, S, D = x.shape
        H = N_HEADS
        dh = D // H
        scale = dh ** (-0.5)
        q = (x @ wq.T + bq).reshape(B, S, H, dh).transpose(0, 2, 1, 3)
        k = (x @ wk.T + bk).reshape(B, S, H, dh).transpose(0, 2, 1, 3)
        v = (x @ wv.T + bv).reshape(B, S, H, dh).transpose(0, 2, 1, 3)
        scores = jnp.einsum('bhqd,bhkd->bhqk', q, k) * scale
        scores = scores + _sliding_window_bias(S)[None, None]
        attn = jax.nn.softmax(scores, axis=-1)
        out = jnp.einsum('bhqk,bhkd->bhqd', attn, v)
        out = out.transpose(0, 2, 1, 3).reshape(B, S, D)
        return out @ wo.T + bo

    def _L1_attn_b_ref(x, Wq, bq, Wk, bk, Wv, bv, Wo, bo):
        import jax, jax.numpy as jnp
        import numpy as np
        HIDDEN = 256
        NUM_HEADS = 16
        NUM_KV = 4
        HEAD_DIM = HIDDEN // NUM_HEADS
        GROUPS = NUM_HEADS // NUM_KV
        SCALE = HEAD_DIM ** 0.5
        B, N, _ = x.shape
        q = x @ Wq + bq
        k = x @ Wk + bk
        v = x @ Wv + bv
        q = q.reshape(B, N, NUM_HEADS, HEAD_DIM).transpose(0, 2, 1, 3)
        q = q.reshape(B, NUM_KV, GROUPS, N, HEAD_DIM).transpose(0, 2, 1, 3, 4)
        k = k.reshape(B, N, NUM_KV, HEAD_DIM).transpose(0, 2, 1, 3)
        v = v.reshape(B, N, NUM_KV, HEAD_DIM).transpose(0, 2, 1, 3)
        scores = jnp.einsum('bghnd,bhsd->bghns', q, k)
        attn = jax.nn.softmax(scores / SCALE, axis=-1)
        out = jnp.einsum('bghns,bhsd->bghnd', attn, v)
        out = out.transpose(0, 3, 1, 2, 4).reshape(B, N, NUM_HEADS * HEAD_DIM)
        return out @ Wo + bo

    def _L1_ffn_ref(x, weight, aux_weight1, aux_weight2, bias):
        import jax, jax.numpy as jnp
        import numpy as np
        D_MODEL = 256
        h = jnp.einsum('btc,cd->btd', x, weight)
        h = jnp.einsum('btc,cd->btd', h, aux_weight1)
        h = jnp.einsum('btc,cd->btd', h, aux_weight2)
        return jnp.tanh(h + bias)
    x = L0_attn_a_out
    x = x + _L0_attn_a_ref(_layernorm(x, axis=-1), L0_attn_a_W_write, L0_attn_a_W_read, L0_attn_a_W_alpha, L0_attn_a_W_beta, L0_attn_a_A_log, L0_attn_a_dt_bias)
    x = x + _L0_ffn_ref(_layernorm(x, axis=-1), L0_ffn_gamma1, L0_ffn_Wq, L0_ffn_bq, L0_ffn_Wdown, L0_ffn_bdown, L0_ffn_Wup, L0_ffn_bup, L0_ffn_Wo, L0_ffn_bo, L0_ffn_gamma2, L0_ffn_Wg, L0_ffn_bg, L0_ffn_We)
    x = x + _L0_attn_b_ref(_layernorm(x, axis=-1), L0_attn_b_Wq, L0_attn_b_Wk, L0_attn_b_Wv, L0_attn_b_Wf, L0_attn_b_Wbet, L0_attn_b_Wo, L0_attn_b_delta, L0_attn_b_lamb_params, L0_attn_b_norm_weight, L0_attn_b_gate_w1, L0_attn_b_gate_w2)
    x = x + _L0_ffn_ref(_layernorm(x, axis=-1), L0_ffn_gamma1, L0_ffn_Wq, L0_ffn_bq, L0_ffn_Wdown, L0_ffn_bdown, L0_ffn_Wup, L0_ffn_bup, L0_ffn_Wo, L0_ffn_bo, L0_ffn_gamma2, L0_ffn_Wg, L0_ffn_bg, L0_ffn_We)
    x = x + _L1_attn_a_ref(_layernorm(x, axis=-1), L1_attn_a_wq, L1_attn_a_bq, L1_attn_a_wk, L1_attn_a_bk, L1_attn_a_wv, L1_attn_a_bv, L1_attn_a_wo, L1_attn_a_bo)
    x = x + _L1_ffn_ref(_layernorm(x, axis=-1), L1_ffn_weight, L1_ffn_aux_weight1, L1_ffn_aux_weight2, L1_ffn_bias)
    x = x + _L1_attn_b_ref(_layernorm(x, axis=-1), L1_attn_b_Wq, L1_attn_b_bq, L1_attn_b_Wk, L1_attn_b_bk, L1_attn_b_Wv, L1_attn_b_bv, L1_attn_b_Wo, L1_attn_b_bo)
    x = x + _L1_ffn_ref(_layernorm(x, axis=-1), L1_ffn_weight, L1_ffn_aux_weight1, L1_ffn_aux_weight2, L1_ffn_bias)
    return x

_drawn_inputs = setup_inputs


def setup_inputs(seed=0):
    import zlib

    import numpy as np

    out = dict(_drawn_inputs(seed))
    spreads = {'L0_attn_a_dt_bias': (1.0, 0.6),
     'L0_attn_b_delta': (4.595119953155518, 0.2),
     'L0_attn_b_lamb_params': (1.9887207746505737, 0.6),
     'L0_attn_b_norm_weight': (1.0, 0.6),
     'L0_ffn_gamma1': (1.0, 0.2),
     'L0_ffn_bq': (0.0, 0.8),
     'L0_ffn_bdown': (0.0, 0.8),
     'L0_ffn_bup': (0.0, 0.308),
     'L0_ffn_bo': (0.0, 0.1),
     'L0_ffn_gamma2': (1.0, 0.2),
     'L0_ffn_bg': (0.0, 0.571),
     'L1_attn_a_bq': (0.0, 0.8),
     'L1_attn_a_bk': (0.0, 2.0),
     'L1_attn_a_bv': (0.0, 0.8),
     'L1_attn_a_bo': (0.0, 0.333),
     'L1_attn_b_bq': (0.0, 0.8),
     'L1_attn_b_bk': (0.0, 2.0),
     'L1_attn_b_bv': (0.0, 0.8),
     'L1_attn_b_bo': (0.0, 0.352),
     'L1_ffn_bias': (0.0, 0.455)}
    factors = {'L0_attn_a_W_write': 8.0,
     'L0_attn_a_W_read': 8.0,
     'L0_attn_a_W_alpha': 8.0,
     'L0_attn_a_W_beta': 8.0,
     'L0_attn_a_A_log': 8.0,
     'L0_attn_b_Wf': 8.0,
     'L0_attn_b_Wbet': 4.742,
     'L0_attn_b_gate_w1': 8.0,
     'L0_attn_b_gate_w2': 8.0,
     'L1_attn_a_wq': 8.0,
     'L1_attn_a_wk': 8.0,
     'L1_attn_a_wv': 8.0,
     'L1_attn_a_wo': 6.815,
     'L1_attn_b_Wq': 8.0,
     'L1_attn_b_Wk': 8.0,
     'L1_attn_b_Wv': 8.0,
     'L1_attn_b_Wo': 7.526,
     'L1_ffn_weight': 3.738,
     'L1_ffn_aux_weight1': 3.735,
     'L1_ffn_aux_weight2': 3.727}
    for name, (base, spread) in spreads.items():
        noise = np.random.default_rng([zlib.crc32(name.encode()), seed]).standard_normal(out[name].shape)
        drawn = base * np.exp(spread * noise) if base else spread * noise
        out[name] = jnp.asarray(drawn.astype(out[name].dtype))
    for name, factor in factors.items():
        out[name] = (out[name] * factor).astype(out[name].dtype)
    return out
```

```python
from contextlib import ExitStack

import numpy as np

import concourse.bass as bass
from concourse import mybir

F32 = mybir.dt.float32
BF16 = mybir.dt.bfloat16
U16 = mybir.dt.uint16
ALU = mybir.AluOpType
ACT = mybir.ActivationFunctionType
AX = mybir.AxisListType.X
P = 128
D = 256
CREDIT = 4


def made(t):
    return t + 1 + CREDIT


def freed(t, n):
    return t + 1 + CREDIT - n


def flat(ap):
    return ap.rearrange("p a d -> p (a d)")


class Scope:

    def __init__(self, nc, name):
        self.nc, self.name, self.ctx, self.sems, self.all_sems = nc, name, ExitStack(), [], []

    def __enter__(self):
        return self

    def __exit__(self, *exc):
        if self.all_sems:
            with self.nc.Block() as block:

                @block.gpsimd
                def _(pool):
                    for s in self.all_sems:
                        pool.sem_clear(s)

        return self.ctx.__exit__(*exc)

    def sb(self, name, shape, dt=F32):
        return self.ctx.enter_context(self.nc.sbuf_tensor(f"{self.name}_{name}", shape, dt))

    def ps(self, name, shape):
        return self.ctx.enter_context(self.nc.psum_tensor(f"{self.name}_{name}", shape, F32))

    def sem(self, name):
        s = self.plain_sem(name)
        self.sems.append(s)
        return s

    def plain_sem(self, name):
        s = self.ctx.enter_context(self.nc.semaphore(f"{self.name}_{name}"))
        self.all_sems.append(s)
        return s

    def arm(self, loads):
        nc = self.nc
        loaded = self.plain_sem("loaded")
        self.settled = self.plain_sem("settled")
        with nc.Block() as block:

            @block.sync
            def _(sp):
                for s in self.sems:
                    sp.sem_inc(s, CREDIT)
                for dst, src in loads:
                    sp.dma_start(dst, src).then_inc(loaded, 16)
                if loads:
                    sp.wait_ge(loaded, 16 * len(loads))

    def settle(self, eng):
        eng.sem_inc(self.settled, 1)


def rows(ap):
    return ap.rearrange("(c p) n -> p c n", p=P)


def spread(ap):
    return ap.partition_broadcast(P)


def tile_of(ap4, g, u):
    return flat(ap4[:, bass.ds(g, 1), u, :])


def normalise(pool, gpsimd, sc, out, x, scale, shift, half, value):
    sc.settle(pool)
    gpsimd.tensor_tensor(out, x, scale.unsqueeze(2).broadcast_to(out.shape), ALU.mult).then_inc(half, 1)
    pool.wait_ge(half, value)
    sc.settle(pool)
    return gpsimd.tensor_tensor(out, out, shift.unsqueeze(2).broadcast_to(out.shape), ALU.add)


def norm_stats(nc, X, NT, rstd, nmr, sc, eps, rms=None, heads=None):
    st = sc.sb("st", [P, 4, 6])
    mv = sc.sb("mv", [P, NT, 2])
    mv4 = sc.sb("mv4", [P, 4, 2])
    tmp = sc.sb("tmp", [P, NT])
    tmp2 = sc.sb("tmp2", [P, NT])
    s_st = sc.plain_sem("st_stats")
    s_mv = sc.plain_sem("st_mv")
    s_pass = sc.plain_sem("st_pass")
    s_ln = sc.plain_sem("st_ln")
    s_rs = sc.plain_sem("st_rstd")
    s_sm = sc.plain_sem("st_small")
    s_r1 = sc.plain_sem("st_r1")
    Xg = X[:, :, :].rearrange("p (g u) d -> p g u d", u=4)
    mg = mv[:, :, :].rearrange("p (g u) d -> p g u d", u=4)
    with nc.Block() as block:

        @block.vector
        def _(dve):
            with dve.Fori(0, NT // 4) as g:
                for u in range(4):
                    nc.vector.bn_stats(st[:, u, :], tile_of(Xg, g, u)).then_inc(s_st, 1)
                for u in range(4):
                    dve.wait_ge(s_st, 4 * g + u + 1)
                    dve.sem_inc(s_pass, 1)
                    nc.vector.bn_aggr(mv4[:, u, :], st[:, u, :]).then_inc(s_mv, 1)
                dve.wait_ge(s_mv, 5 * g + 4)
                nc.vector.tensor_copy(mg[:, bass.ds(g, 1), :, :], mv4[:, :, :].unsqueeze(1)).then_inc(s_mv, 1)
                dve.wait_ge(s_mv, 5 * g + 5)
            dve.wait_ge(s_rs, 1)
            nc.vector.scalar_tensor_tensor(out=nmr[:, :], in0=mv[:, :, 0], scalar=-1.0, in1=rstd[:, :],
                                           op0=ALU.mult, op1=ALU.mult).then_inc(s_sm, 1)
            if rms is not None:
                nc.vector.tensor_tensor(tmp[:, :], rstd[:, :], rstd[:, :], ALU.mult).then_inc(s_sm, 1)
                dve.wait_ge(s_sm, 2)
                nc.vector.tensor_tensor(tmp2[:, :], tmp[:, :], mv[:, :, 1], ALU.mult).then_inc(s_sm, 1)
                dve.wait_ge(s_r1, 2)
                hs, hn = rms
                nc.vector.tensor_tensor(hs[:, :], rstd[:, :], tmp[:, :], ALU.mult).then_inc(s_sm, 1)
                nc.vector.tensor_tensor(hn[:, :], nmr[:, :], tmp[:, :], ALU.mult).then_inc(s_sm, 1)

        @block.scalar
        def _(act):
            act.wait_ge(s_mv, NT // 4 * 5)
            nc.scalar.activation(rstd[:, :], mv[:, :, 1], ACT.Ln, bias=eps[:, 0:1]).then_inc(s_ln, 1)
            act.wait_ge(s_ln, 1)
            nc.scalar.activation(rstd[:, :], rstd[:, :], ACT.Exp, scale=-0.5).then_inc(s_rs, 1)
            if rms is not None:
                act.wait_ge(s_sm, 3)
                nc.scalar.activation(tmp2[:, :], tmp2[:, :], ACT.Ln, bias=eps[:, 1:2]).then_inc(s_r1, 1)
                act.wait_ge(s_r1, 1)
                nc.scalar.activation(tmp[:, :], tmp2[:, :], ACT.Exp, scale=-0.5).then_inc(s_r1, 1)


def pair_views(X, rstd, nmr):
    return (X[:, :, :].rearrange("p (g v k) d -> p g v (k d)", v=2, k=2),
            *[a[:, :].rearrange("p (g v k) -> p g v k", v=2, k=2) for a in (rstd, nmr)])


def twice(ap):
    return ap.unsqueeze(1).broadcast_to([ap.shape[0], 2, ap.shape[1]])


def by_tile(ap):
    return ap.rearrange("p (k d) -> p k d", k=2)


def at(ap4, g, v):
    return flat(ap4[:, bass.ds(g, 1), v, :])


def linear3_tanh(nc, X, NT, name, w, ident, eps):
    with Scope(nc, name) as sc:
        W0T = sc.sb("W0T", [P, 2, D])
        A1 = sc.sb("A1", [P, 2, D])
        A2 = sc.sb("A2", [P, 2, D])
        WAT = sc.sb("WAT", [P, 2, D])
        W = sc.sb("W", [P, 2, D])
        bias = sc.sb("bias", [P, D])
        rstd = sc.sb("rstd", [P, NT])
        nmr = sc.sb("nmr", [P, NT])
        xl = sc.sb("xl", [P, 2, 2, D])
        xT = sc.sb("xT", [P, 2, 4 * P])
        z = sc.sb("z", [P, 2, 2 * D])
        th = sc.sb("th", [P, 2, 2 * D])
        psT = [sc.ps(f"psT{i}", [P, 4 * P]) for i in range(2)]
        psY = [sc.ps(f"psY{i}", [P, 2 * D]) for i in range(2)]
        psW = sc.ps("psW", [P, 2, D])
        s_xl, s_T, s_xT, s_y, s_z, s_th, s_x = [sc.sem(n) for n in
                                                ("xl", "T", "xT", "y", "z", "th", "x")]
        s_xh = sc.sem("xh")
        s_w = sc.plain_sem("w")
        s_wc = sc.plain_sem("wc")
        sc.arm([(W0T[:, :, :], rows(w["weightT"])), (A1[:, :, :], rows(w["aux1"])),
                (A2[:, :, :], rows(w["aux2"])), (bias[:, :], spread(w["bias"]))])
        norm_stats(nc, X, NT, rstd, nmr, sc, eps)
        Xp, rp, mp = pair_views(X, rstd, nmr)
        G = NT // 4
        with nc.Block() as block:

            @block.gpsimd
            def _(pool):
                with pool.Fori(0, G) as g:
                    for v in range(2):
                        n = 2 * g + v
                        pool.wait_ge(s_T, freed(n, 2))
                        normalise(pool, nc.gpsimd, sc, xl[:, v, :, :], by_tile(at(Xp, g, v)), at(rp, g, v), at(mp, g, v),
                                  s_xh, made(n)).then_inc(s_xl, 1)

            @block.tensor
            def _(pe):
                for m in range(2):
                    for k in range(2):
                        i = nc.tensor.matmul(psW[:, m, :], A1[:, k, m * P:(m + 1) * P], W0T[:, k, :],
                                             start=(k == 0), stop=(k == 1))
                i.then_inc(s_w, 1)
                pe.wait_ge(s_wc, 1)
                for m in range(2):
                    for k in range(2):
                        i = nc.tensor.matmul(psW[:, m, :], WAT[:, k, m * P:(m + 1) * P], A2[:, k, :],
                                             start=(k == 0), stop=(k == 1))
                i.then_inc(s_w, 1)
                pe.wait_ge(s_wc, 2)
                with pe.Fori(0, G) as g:
                    for v in range(2):
                        n = 2 * g + v
                        pe.wait_ge(s_xl, made(n))
                        pe.wait_ge(s_xT, freed(n, 2))
                        for k in range(2):
                            for c in range(2):
                                i = nc.tensor.transpose(psT[v][:, (2 * k + c) * P:(2 * k + c + 1) * P],
                                                        xl[:, v, k, c * P:(c + 1) * P], ident[:, :])
                        i.then_inc(s_T, 1)
                    for v in range(2):
                        n = 2 * g + v
                        pe.wait_ge(s_xT, made(n))
                        pe.wait_ge(s_z, freed(n, 2))
                        for k in range(2):
                            for c in range(2):
                                i = nc.tensor.matmul(psY[v][:, k * D:(k + 1) * D],
                                                     xT[:, v, (2 * k + c) * P:(2 * k + c + 1) * P], W[:, c, :],
                                                     start=(c == 0), stop=(c == 1))
                        i.then_inc(s_y, 1)

            @block.scalar
            def _(act):
                act.wait_ge(s_w, 1)
                nc.scalar.activation(WAT[:, :, :], psW[:, :, :], ACT.Copy).then_inc(s_wc, 1)
                act.wait_ge(s_w, 2)
                nc.scalar.activation(W[:, :, :], psW[:, :, :], ACT.Copy).then_inc(s_wc, 1)
                with act.Fori(0, G) as g:
                    for v in range(2):
                        n = 2 * g + v
                        act.wait_ge(s_T, made(n))
                        act.wait_ge(s_y, freed(n, 2))
                        nc.scalar.activation(xT[:, v, :], psT[v][:, :], ACT.Copy).then_inc(s_xT, 1)
                    for v in range(2):
                        n = 2 * g + v
                        act.wait_ge(s_z, made(n))
                        act.wait_ge(s_x, freed(n, 2))
                        nc.scalar.activation(th[:, v, :], z[:, v, :], ACT.Tanh).then_inc(s_th, 1)

            @block.vector
            def _(dve):
                with dve.Fori(0, G) as g:
                    for v in range(2):
                        n = 2 * g + v
                        dve.wait_ge(s_y, made(n))
                        dve.wait_ge(s_th, freed(n, 2))
                        nc.vector.tensor_tensor(by_tile(z[:, v, :]), by_tile(psY[v][:, :]), twice(bias[:, :]),
                                                ALU.add).then_inc(s_z, 1)
                    for v in range(2):
                        n = 2 * g + v
                        dve.wait_ge(s_th, made(n))
                        dve.wait_ge(s_xl, made(n))
                        nc.vector.tensor_tensor(at(Xp, g, v), at(Xp, g, v), th[:, v, :], ALU.add).then_inc(s_x, 1)


HEADS = 16
HD = D // HEADS
RANK = 64
EXPERTS = 8


def token_ffn(nc, X, NT, name, w, ident, eps):
    E, H = EXPERTS, HEADS
    HH = H // 2
    with Scope(nc, name) as sc:
        Wq = sc.sb("Wq", [P, 2, D])
        Wd = sc.sb("Wd", [P, 2, RANK])
        Wu = sc.sb("Wu", [P, 2 * D])
        Wo = sc.sb("Wo", [P, 2, D])
        Wg = sc.sb("Wg", [P, 2, E])
        We = sc.sb("We", [P, 2, E, D])
        gam = sc.sb("gam", [P, 2, 2])
        bq = sc.sb("bq", [P, D])
        bd = sc.sb("bd", [RANK, 1])
        bo = sc.sb("bo", [P, D])
        bg = sc.sb("bg", [P, E])
        rstd = sc.sb("rstd", [P, NT])
        nmr = sc.sb("nmr", [P, NT])
        hsc = sc.sb("hsc", [P, NT])
        hnm = sc.sb("hnm", [P, NT])
        hn = sc.sb("hn", [P, 2, 2, D])
        xl = sc.sb("xl", [P, 2, 2 * D])
        hT = sc.sb("hT", [P, 4 * P])
        dT = sc.sb("dT", [P, 2 * P])
        q = sc.sb("q", [P, 2 * D])
        kv = sc.sb("kv", [P, 2, 2 * D])
        prod = sc.sb("prod", [P, 2, H, H * HD])
        att = sc.sb("att", [P, 2, H * H])
        mx = sc.sb("mx", [P, 2, H])
        rs = sc.sb("rs", [P, 2, H])
        out = sc.sb("out", [P, 2 * D])
        oT = sc.sb("oT", [P, 4 * P])
        x1 = sc.sb("x1", [P, 2 * D])
        sq = sc.sb("sq", [P, 2, D])
        ss = sc.sb("ss", [P, 2])
        r2 = sc.sb("r2", [P, 2])
        h2 = sc.sb("h2", [P, 2 * D])
        h2T = sc.sb("h2T", [P, 4 * P])
        gl = sc.sb("gl", [P, 2, E])
        gm = sc.sb("gm", [P, 2])
        gs = sc.sb("gs", [P, 2])
        gr = sc.sb("gr", [P, 2])
        ex = sc.sb("ex", [P, E, 2 * D])
        psT = sc.ps("psT", [P, 4 * P])
        psQ = sc.ps("psQ", [P, 2 * D])
        psKV = [sc.ps(f"psKV{i}", [P, 2 * D]) for i in range(2)]
        psD = sc.ps("psD", [P, 4 * P])
        psO = sc.ps("psO", [P, 2 * D])
        psE = [sc.ps(f"psE{i}", [P, 2 * D]) for i in range(2)]
        (s_hn, s_xl, s_xlb, s_T1, s_hT, s_q, s_d, s_dT, s_kv, s_kvs, s_qs, s_pA, s_pAd, s_rA, s_mx, s_sub, s_ex,
         s_sum, s_rec, s_pB, s_pBd, s_rB, s_out, s_T2, s_oT, s_o, s_x1, s_sq, s_ln, s_r2, s_h2, s_T3, s_h2T, s_g,
         s_gl, s_gm, s_ge, s_gr, s_gn, s_e, s_es, s_xx, s_a1, s_a2, s_a3, s_xo) = [sc.sem(n) for n in (
             "hn", "xl", "xlb", "T1", "hT", "q", "d", "dT", "kv", "kvs", "qs", "pA", "pAd", "rA", "mx", "sub",
             "ex", "sum", "rec", "pB", "pBd", "rB", "out", "T2", "oT", "o", "x1", "sq", "ln", "r2", "h2", "T3",
             "h2T", "g", "gl", "gm", "ge", "gr", "gn", "e", "es", "xx", "a1", "a2", "a3", "xo")]
        s_zero = sc.plain_sem("zero")
        s_fold = sc.plain_sem("fold")
        with nc.Block() as block:

            @block.vector
            def _(dve):
                nc.vector.memset(Wu[:, :], 0.0).then_inc(s_zero, 1)
                nc.vector.memset(dT[:, :], 0.0).then_inc(s_zero, 1)
                dve.wait_ge(s_zero, 2)
                nc.vector.memset(dT[RANK:RANK + 1, :], 1.0).then_inc(s_zero, 1)

        sc.arm([(Wq[:, :, :], rows(w["Wq"])), (Wd[:, :, :], rows(w["Wdown"])), (Wu[0:RANK, :], w["Wup"]),
                (Wu[RANK:RANK + 1, :], w["bup"].unsqueeze(0)), (Wo[:, :, :], rows(w["Wo"])), (Wg[:, :, :], rows(w["Wg"])),
                *[(We[:, c, :, :], w["We"][:, c * P:(c + 1) * P, :].rearrange("e p n -> p e n")) for c in range(2)],
                (gam[:, :, :], w["gammas"]),
                (bq[:, :], spread(w["bq"])), (bd[:, :], w["bdown"].unsqueeze(1)), (bo[:, :], spread(w["bo"])),
                (bg[:, :], spread(w["bg"]))])
        norm_stats(nc, X, NT, rstd, nmr, sc, eps, rms=(hsc, hnm))
        Xp, rp, mp = pair_views(X, rstd, nmr)
        hp, kp = pair_views(X, hsc, hnm)[1:]
        G = NT // 4

        def scores_product(eng, k, half):
            hs = slice(half * HH, half * HH + HH)
            o = prod[:, k, hs, :].rearrange("p h (g d) -> p h g d", d=HD)
            a = q[:, k * D:(k + 1) * D].rearrange("p (h d) -> p h d", d=HD)[:, hs, :].unsqueeze(2)
            b = kv[:, k, :].rearrange("p (g s d) -> p g s d", s=2, d=HD)[:, :, 0, :].unsqueeze(1)
            return eng.tensor_tensor(o, a.broadcast_to([P, HH, H, HD]), b.broadcast_to([P, HH, H, HD]), ALU.mult)

        def values_product(eng, k, half):
            hs = slice(half * HH, half * HH + HH)
            o = prod[:, k, hs, :].rearrange("p h (d g) -> p h d g", g=H)
            a = att[:, k, :].rearrange("p (h g) -> p h g", g=H)[:, hs, :].unsqueeze(2)
            b = kv[:, k, :].rearrange("p (g s d) -> p d s g", s=2, d=HD)[:, :, 1, :].unsqueeze(1)
            return eng.tensor_tensor(o, a.broadcast_to([P, HH, HD, H]), b.broadcast_to([P, HH, HD, H]), ALU.mult)

        with nc.Block() as block:

            @block.gpsimd
            def _(pool):
                for c in range(2):
                    for m, j in ((Wq[:, c, :], 0), (Wd[:, c, :], 0), (Wg[:, c, :], 1),
                                 (We[:, c, :, :].rearrange("p e n -> p (e n)"), 1)):
                        nc.gpsimd.tensor_scalar(m, m, gam[:, c, j:j + 1], 1.0, ALU.mult, ALU.mult).then_inc(s_fold, 1)

                def mix(g, v):
                    n = 2 * g + v
                    for k in range(2):
                        t = 2 * n + k
                        pool.wait_ge(s_qs, made(n))
                        pool.wait_ge(s_kvs, made(t))
                        pool.wait_ge(s_rB, freed(t, 2))
                        scores_product(nc.gpsimd, k, 0).then_inc(s_pA, 1)
                    for k in range(2):
                        t = 2 * n + k
                        pool.wait_ge(s_ex, made(t))
                        pool.wait_ge(s_rA, made(t))
                        values_product(nc.gpsimd, k, 0).then_inc(s_pB, 1)
                    pool.wait_ge(s_xl, made(n))
                    nc.gpsimd.tensor_tensor(by_tile(xl[:, v, :]), by_tile(xl[:, v, :]), twice(bo[:, :]),
                                            ALU.add).then_inc(s_xlb, 1)

                def back(g, v):
                    n = 2 * g + v
                    pool.wait_ge(s_es, made(16 * n + 15))
                    nc.gpsimd.tensor_tensor(ex[:, 0:4, :], ex[:, 0:4, :], ex[:, 4:8, :], ALU.add).then_inc(s_a1, 1)
                    pool.wait_ge(s_a1, made(n))
                    nc.gpsimd.tensor_tensor(ex[:, 0:2, :], ex[:, 0:2, :], ex[:, 2:4, :], ALU.add).then_inc(s_a2, 1)
                    pool.wait_ge(s_a2, made(n))
                    nc.gpsimd.tensor_tensor(ex[:, 0, :], ex[:, 0, :], ex[:, 1, :], ALU.add).then_inc(s_a3, 1)
                    pool.wait_ge(s_a3, made(n))
                    pool.wait_ge(s_xx, made(n))
                    nc.gpsimd.tensor_tensor(at(Xp, g, v), at(Xp, g, v), ex[:, 0, :], ALU.add).then_inc(s_xo, 1)

                mix(0, 0)
                with pool.Fori(0, G - 1) as g:
                    mix(g, 1)
                    back(g, 0)
                    mix(g + 1, 0)
                    back(g, 1)
                mix(G - 1, 1)
                back(G - 1, 0)
                back(G - 1, 1)

            @block.tensor
            def _(pe):
                def transposes(src, s_src, n, s_free, s_done):
                    pe.wait_ge(s_src, made(n))
                    pe.wait_ge(*s_free)
                    for j in range(4):
                        i = nc.tensor.transpose(psT[:, j * P:(j + 1) * P], src[:, j * P:(j + 1) * P], ident[:, :])
                    i.then_inc(s_done, 1)

                def front(g, v):
                    n = 2 * g + v
                    transposes(hn[:, v, :, :].rearrange("p k d -> p (k d)"), s_hn, n, (s_h2T, freed(n, 1) - 1), s_T1)
                    pe.wait_ge(s_hT, made(n))
                    pe.wait_ge(s_qs, freed(n, 1))
                    for k in range(2):
                        for c in range(2):
                            i = nc.tensor.matmul(psQ[:, k * D:(k + 1) * D], hT[:, (2 * k + c) * P:(2 * k + c + 1) * P],
                                                 Wq[:, c, :], start=(c == 0), stop=(c == 1))
                    i.then_inc(s_q, 1)
                    pe.wait_ge(s_gl, freed(n, 1) - 1)
                    hTv = hT[:, :].rearrange("p (k c t) -> p c k t", k=2, c=2)
                    for c in range(2):
                        i = nc.tensor.matmul(psD[0:RANK, 0:2 * P].rearrange("p (k t) -> p k t", k=2), Wd[:, c, :],
                                             hTv[:, c, :, :], start=(c == 0), stop=(c == 1))
                    i.then_inc(s_d, 1)
                    pe.wait_ge(s_dT, made(n))
                    for k in range(2):
                        pe.wait_ge(s_kvs, freed(2 * n + k, 2))
                        nc.tensor.matmul(psKV[k][:, :], dT[:, k * P:(k + 1) * P], Wu[:, :], start=True,
                                         stop=True).then_inc(s_kv, 1)

                def back(g, v, last=False):
                    n = 2 * g + v
                    ahead = 0 if last else 1
                    transposes(out, s_out, n, (s_hT, made(n) + ahead), s_T2)
                    pe.wait_ge(s_oT, made(n))
                    pe.wait_ge(s_x1, freed(n, 1))
                    pe.wait_ge(s_sq, freed(n, 1))
                    pe.wait_ge(s_xlb, made(n))
                    nc.tensor.matmul(psO[:, :], ident[:, :], xl[:, v, :], start=True, stop=False, skip_group_check=True)
                    for k in range(2):
                        for c in range(2):
                            i = nc.tensor.matmul(psO[:, k * D:(k + 1) * D], oT[:, (2 * k + c) * P:(2 * k + c + 1) * P],
                                                 Wo[:, c, :], start=False, stop=(c == 1), skip_group_check=True)
                    i.then_inc(s_o, 1)
                    transposes(h2, s_h2, n, (s_oT, made(n)), s_T3)
                    pe.wait_ge(s_h2T, made(n))
                    pe.wait_ge(s_dT, made(n) + ahead)
                    for k in range(2):
                        for c in range(2):
                            i = nc.tensor.matmul(psD[:, 256 + k * E:256 + (k + 1) * E],
                                                 h2T[:, (2 * k + c) * P:(2 * k + c + 1) * P],
                                                 Wg[:, c, :], start=(c == 0), stop=(c == 1))
                    i.then_inc(s_g, 1)
                    for k in range(2):
                        for e in range(0, E, 2):
                            b = 16 * n + 8 * k + e
                            pe.wait_ge(s_es, freed(b + 1, 4))
                            for c in range(2):
                                i = nc.tensor.matmul(psE[e // 2 % 2][:, :], h2T[:, (2 * k + c) * P:(2 * k + c + 1) * P],
                                                     We[:, c, e:e + 2, :].rearrange("p e n -> p (e n)"),
                                                     start=(c == 0), stop=(c == 1))
                            i.then_inc(s_e, 1)

                pe.wait_ge(s_fold, 8)
                front(0, 0)
                with pe.Fori(0, G - 1) as g:
                    front(g, 1)
                    back(g, 0)
                    front(g + 1, 0)
                    back(g, 1)
                front(G - 1, 1)
                back(G - 1, 0)
                back(G - 1, 1, last=True)

            @block.scalar
            def _(act):
                def norm(g, v):
                    act.wait_ge(s_T1, freed(2 * g + v, 2))
                    sc.settle(act)
                    for k in range(2):
                        i = nc.scalar.activation(hn[:, v, k, :], at(Xp, g, v)[:, k * D:(k + 1) * D], ACT.Identity,
                                                 scale=hp[:, bass.ds(g, 1), v, k], bias=kp[:, bass.ds(g, 1), v, k])
                    i.then_inc(s_hn, 1)

                def front(g, v):
                    n = 2 * g + v
                    act.wait_ge(s_T1, made(n))
                    act.wait_ge(s_d, freed(n, 1))
                    nc.scalar.activation(hT[:, :], psT[:, :], ACT.Copy).then_inc(s_hT, 1)
                    act.wait_ge(s_d, made(n))
                    act.wait_ge(s_kv, freed(2 * n + 1, 2))
                    nc.scalar.activation(dT[0:RANK, :], psD[0:RANK, 0:2 * P], ACT.Identity,
                                         bias=bd[:, 0:1]).then_inc(s_dT, 1)
                    for k in range(2):
                        t = 2 * n + k
                        act.wait_ge(s_kv, made(t))
                        act.wait_ge(s_rB, freed(t, 2))
                        nc.scalar.activation(kv[:, k, :], psKV[k][:, :], ACT.Copy).then_inc(s_kvs, 1)
                    act.wait_ge(s_o, freed(n, 2))
                    sc.settle(act)
                    for k in range(2):
                        i = nc.scalar.activation(xl[:, v, k * D:(k + 1) * D], at(Xp, g, v)[:, k * D:(k + 1) * D],
                                                 ACT.Identity, scale=rp[:, bass.ds(g, 1), v, k],
                                                 bias=mp[:, bass.ds(g, 1), v, k])
                    i.then_inc(s_xl, 1)

                def exps(g, v, k):
                    t = 2 * (2 * g + v) + k
                    act.wait_ge(s_sub, made(t))
                    nc.scalar.activation(att[:, k, :], att[:, k, :], ACT.Exp, scale=HD ** -0.5).then_inc(s_ex, 1)

                def back(g, v):
                    n = 2 * g + v
                    act.wait_ge(s_T2, made(n))
                    act.wait_ge(s_o, freed(n, 1))
                    nc.scalar.activation(oT[:, :], psT[:, :], ACT.Copy).then_inc(s_oT, 1)
                    act.wait_ge(s_o, made(n))
                    act.wait_ge(s_xx, freed(n, 1))
                    act.wait_ge(s_r2, freed(n, 1))
                    act.wait_ge(s_h2, freed(n, 1))
                    nc.scalar.activation(x1[:, :], psO[:, :], ACT.Copy).then_inc(s_x1, 1)
                    for k in range(2):
                        i = nc.scalar.activation(sq[:, k, :], psO[:, k * D:(k + 1) * D], ACT.Square,
                                                 accum_out=ss[:, k:k + 1])
                    i.then_inc(s_sq, 1)
                    act.wait_ge(s_sq, made(n))
                    nc.scalar.activation(r2[:, :], ss[:, :], ACT.Ln, scale=1.0 / D, bias=eps[:, 1:2]).then_inc(s_ln, 1)
                    act.wait_ge(s_ln, made(n))
                    nc.scalar.activation(r2[:, :], r2[:, :], ACT.Exp, scale=-0.5).then_inc(s_r2, 1)
                    act.wait_ge(s_r2, made(n))
                    act.wait_ge(s_x1, made(n))
                    act.wait_ge(s_T3, freed(n, 1))
                    for k in range(2):
                        i = nc.scalar.activation(h2[:, k * D:(k + 1) * D], x1[:, k * D:(k + 1) * D], ACT.Copy,
                                                 scale=r2[:, k:k + 1])
                    i.then_inc(s_h2, 1)
                    act.wait_ge(s_T3, made(n))
                    act.wait_ge(s_e, freed(8 * n + 7, 8))
                    nc.scalar.activation(h2T[:, :], psT[:, :], ACT.Copy).then_inc(s_h2T, 1)

                def gate_exps(g, v):
                    n = 2 * g + v
                    act.wait_ge(s_gm, made(n))
                    act.wait_ge(s_gr, freed(n, 1))
                    for k in range(2):
                        i = nc.scalar.activation(gl[:, k, :], gl[:, k, :], ACT.Exp, bias=gm[:, k:k + 1],
                                                 accum_out=gs[:, k:k + 1])
                    i.then_inc(s_ge, 1)

                def experts(g, v):
                    n = 2 * g + v
                    act.wait_ge(s_gn, made(n))
                    act.wait_ge(s_xo, freed(n, 1))
                    for k in range(2):
                        for e in range(E):
                            act.wait_ge(s_e, made(8 * n + 4 * k + e // 2))
                            nc.scalar.activation(ex[:, e, k * D:(k + 1) * D], psE[e // 2 % 2][:, e % 2 * D:(e % 2 + 1) * D],
                                                 ACT.Copy, scale=gl[:, k, e:e + 1]).then_inc(s_es, 1)

                def step(g, v, g1, v1, ahead=None):
                    front(g1, v1)
                    if ahead is not None:
                        norm(ahead, v)
                    back(g, v)
                    exps(g1, v1, 0)
                    gate_exps(g, v)
                    exps(g1, v1, 1)
                    experts(g, v)

                norm(0, 0)
                norm(0, 1)
                front(0, 0)
                exps(0, 0, 0)
                exps(0, 0, 1)
                with act.Fori(0, G - 1) as g:
                    step(g, 0, g, 1, g + 1)
                    step(g, 1, g + 1, 0, g + 1)
                step(G - 1, 0, G - 1, 1)
                back(G - 1, 1)
                gate_exps(G - 1, 1)
                experts(G - 1, 1)

            @block.vector
            def _(dve):
                def front(g, v):
                    n = 2 * g + v
                    dve.wait_ge(s_q, made(n))
                    dve.wait_ge(s_pA, freed(2 * n + 1, 2))
                    nc.vector.tensor_tensor(by_tile(q[:, :]), by_tile(psQ[:, :]), twice(bq[:, :]),
                                            ALU.add).then_inc(s_qs, 1)

                def scores(g, v, k):
                    n = 2 * g + v
                    t = 2 * n + k
                    dve.wait_ge(s_qs, made(n))
                    dve.wait_ge(s_kvs, made(t))
                    scores_product(nc.vector, k, 1).then_inc(s_pAd, 1)

                def scores_sum(g, v, k):
                    t = 2 * (2 * g + v) + k
                    a = att[:, k, :].rearrange("p (h g) -> p h g", g=H)
                    dve.wait_ge(s_pAd, made(t))
                    dve.wait_ge(s_pA, made(t))
                    nc.vector.tensor_reduce(att[:, k, :], prod[:, k, :, :].rearrange("p h (g d) -> p (h g) d", d=HD),
                                            AX, ALU.add).then_inc(s_rA, 1)
                    dve.wait_ge(s_rA, made(t))
                    nc.vector.tensor_reduce(mx[:, k, :], a, AX, ALU.max).then_inc(s_mx, 1)
                    dve.wait_ge(s_mx, made(t))
                    nc.vector.tensor_tensor(a, a, mx[:, k, :].unsqueeze(2).broadcast_to([P, H, H]),
                                            ALU.subtract).then_inc(s_sub, 1)

                def values(g, v, k):
                    t = 2 * (2 * g + v) + k
                    dve.wait_ge(s_ex, made(t))
                    dve.wait_ge(s_rA, made(t))
                    values_product(nc.vector, k, 1).then_inc(s_pBd, 1)
                    nc.vector.tensor_reduce(rs[:, k, :], att[:, k, :].rearrange("p (h g) -> p h g", g=H), AX,
                                            ALU.add).then_inc(s_sum, 1)
                    dve.wait_ge(s_sum, made(t))
                    nc.vector.reciprocal(rs[:, k, :], rs[:, k, :]).then_inc(s_rec, 1)

                def values_sum(g, v, k):
                    n = 2 * g + v
                    t = 2 * n + k
                    dve.wait_ge(s_pBd, made(t))
                    dve.wait_ge(s_pB, made(t))
                    dve.wait_ge(s_T2, freed(n, 1))
                    o = out[:, k * D:(k + 1) * D]
                    nc.vector.tensor_reduce(o, prod[:, k, :, :].rearrange("p h (d g) -> p (h d) g", g=H), AX,
                                            ALU.add).then_inc(s_rB, 1)
                    dve.wait_ge(s_rB, made(t))
                    dve.wait_ge(s_rec, made(t))
                    ov = o.rearrange("p (h d) -> p h d", d=HD)
                    i = nc.vector.tensor_tensor(ov, ov, rs[:, k, :].unsqueeze(2).broadcast_to([P, H, HD]), ALU.mult)
                    if k == 1:
                        i.then_inc(s_out, 1)

                def gate_max(g, v):
                    n = 2 * g + v
                    dve.wait_ge(s_g, made(n))
                    dve.wait_ge(s_es, freed(16 * n + 15, 16))
                    nc.vector.tensor_tensor(gl[:, :, :], psD[:, 256:256 + 2 * E].rearrange("p (k e) -> p k e", k=2),
                                            twice(bg[:, :]), ALU.add).then_inc(s_gl, 1)
                    dve.wait_ge(s_gl, made(n))
                    nc.vector.tensor_reduce(gm[:, :], gl[:, :, :], AX, ALU.max, negate=True).then_inc(s_gm, 1)

                def gate_norm(g, v):
                    n = 2 * g + v
                    dve.wait_ge(s_ge, made(n))
                    nc.vector.reciprocal(gr[:, :], gs[:, :]).then_inc(s_gr, 1)
                    dve.wait_ge(s_gr, made(n))
                    nc.vector.tensor_tensor(gl[:, :, :], gl[:, :, :], gr[:, :].unsqueeze(2).broadcast_to([P, 2, E]),
                                            ALU.mult).then_inc(s_gn, 1)

                def add_y1(g, v):
                    n = 2 * g + v
                    dve.wait_ge(s_x1, made(n))
                    dve.wait_ge(s_xlb, made(n))
                    nc.vector.tensor_tensor(at(Xp, g, v), at(Xp, g, v), x1[:, :], ALU.add).then_inc(s_xx, 1)

                def step(g, v, g1, v1):
                    front(g1, v1)
                    scores(g1, v1, 0)
                    scores_sum(g1, v1, 0)
                    gate_max(g, v)
                    scores(g1, v1, 1)
                    gate_norm(g, v)
                    scores_sum(g1, v1, 1)
                    values(g1, v1, 0)
                    add_y1(g, v)
                    values_sum(g1, v1, 0)
                    values(g1, v1, 1)
                    values_sum(g1, v1, 1)

                front(0, 0)
                for k in range(2):
                    scores(0, 0, k)
                    scores_sum(0, 0, k)
                for k in range(2):
                    values(0, 0, k)
                    values_sum(0, 0, k)
                with dve.Fori(0, G - 1) as g:
                    step(g, 0, g, 1)
                    step(g, 1, g + 1, 0)
                step(G - 1, 0, G - 1, 1)
                gate_max(G - 1, 1)
                gate_norm(G - 1, 1)
                add_y1(G - 1, 1)


KEYS_WINDOW = 64
STACK = 6 * HD
Q_PARTS = (0, 0, 0, 1, 1, 2)
K_PARTS = (0, 1, 2, 0, 1, 0)


def done_before(b, per_batch):
    return b * per_batch + CREDIT


def attention(nc, X, B, T, name, w, ident, identb, eps, local):
    NQ = T // P
    NP2 = NQ // 2
    KVH = 16 if local else 4
    PAD = KEYS_WINDOW if local else 0
    TK = T + 2 * PAD
    NV = TK // P
    nK = (KVH // 8 if local else 1) * (T // 512)
    nQ = 2 * (T // 512)
    R = nK + nQ
    KROWS = P if local else KVH * HD
    KH = 8 if local else 4
    H = HEADS
    steps = ([(True, m, tb) for m in range(2 if local else 1) for tb in range(T // 512)]
             + [(False, m, tb) for m in range(2) for tb in range(T // 512)])
    stacks = [(r, h) for r, (isk, _, _) in enumerate(steps) for h in range(KH if isk else 8)]
    NS2 = len(stacks) // 2
    NMX = NQ * 8 if local else NQ * H * 2
    NU = NQ * 8 if local else (T // 512) * (T // 256) * H
    NG = NQ if local else 4 * (T // 512)
    NAV = NU // 2 if local else NU // 4
    NY = NQ if local else NQ // 2
    with Scope(nc, name + "n") as stats, Scope(nc, name) as sc:
        rstd = stats.sb("rstd", [P, B * NQ])
        nmr = stats.sb("nmr", [P, B * NQ])
        with Scope(nc, name + "t") as temporary:
            norm_stats(nc, X, B * NQ, rstd, nmr, temporary, eps)
        Wq = sc.sb("Wq", [P, 2, D])
        Wk = sc.sb("Wk", [P, 2, KVH * HD])
        Wv = sc.sb("Wv", [P, 2, KVH * HD])
        Wo = sc.sb("Wo", [P, 4, D])
        qb = sc.sb("qb", [P, 2])
        kb = sc.sb("kb", [P, 2])
        bv = sc.sb("bv", [P, KVH * HD])
        bo = sc.sb("bo", [P, D])
        selq = sc.sb("selq", [P, 3, 8, STACK], BF16)
        selk = sc.sb("selk", [P, 3, 8, STACK], BF16)
        sels = sc.sb("sels", [P, P])
        minus = sc.sb("minus", [P, H], BF16)
        xl = sc.sb("xl", [P, 2, 2 * D])
        xT = sc.sb("xT", [P, 2, TK])
        f = sc.sb("f", [P, 2, 512])
        parts = sc.sb("parts", [P, 2, 3, 512], BF16)
        QS = sc.sb("QS", [P, H, T], BF16)
        KS = sc.sb("KS", [P, H, TK], BF16)
        V = sc.sb("V", [P, NV, KVH, 32])
        mx = sc.sb("mx", [P, 2, H, 2])
        m1 = sc.sb("m1", [P, 2, H])
        mb = sc.sb("mb", [P, 2, P], BF16)
        prob = sc.sb("prob", [P, 2, 4, 1024 if not local else 256])
        O, Rc = f[:, 0, :], f[:, 1, :]
        On = xT[:, 0:1, PAD:PAD + 512] if local else xT[:, :, 0:1024].rearrange("p c (a n) -> p (c a) n", n=512)
        if local:
            mask = sc.sb("mask", [P, 3, 256], BF16)
            maskT = sc.sb("maskT", [P, 3, 256], BF16)
        bk = [sc.ps(f"bk{i}", [P, 512]) for i in range(4)]
        bS = [sc.ps(f"bS{i}", [P, 1024]) for i in range(2)]
        bs4 = [bS[0][:, 0:512], bS[0][:, 512:1024], bS[1][:, 0:512], bS[1][:, 512:1024]]
        (s_xl, s_xb, s_T, s_xT, s_f, s_fs, s_sp, s_spq, s_st, s_ka, s_kd, s_v, s_vs, s_m, s_mx, s_m1, s_mh, s_mb,
         s_mT, s_qm, s_s, s_e, s_av, s_os, s_sum, s_rc, s_on, s_y, s_xo) = [sc.sem(n) for n in (
             "xl", "xb", "T", "xT", "f", "fs", "sp", "spq", "st", "ka", "kd", "v", "vs", "m", "mx", "m1", "mh",
             "mb", "mT", "qm", "s", "e", "av", "os", "sum", "rc", "on", "y", "xo")]
        s_zero = sc.plain_sem("zero")
        s_xh = sc.sem("xh")
        loads = [(Wq[:, :, :], rows(w["wq"])), (Wk[:, :, :], rows(w["wk"])), (Wv[:, :, :], rows(w["wv"])),
                 (Wo[:, :, :], w["wo"]), (qb[:, :], w["bq"]), (kb[0:KROWS, 0:2 if local else 1], w["bk"]),
                 (bv[:, :], spread(w["bv"])), (bo[:, :], spread(w["bo"])), (selq[:, :, :, :].bitcast(U16), w["selq"]),
                 (selk[:, :, :, :].bitcast(U16), w["selk"]), (sels[:, :], w["sels"]), (minus[:, :].bitcast(U16), w["minus"])]
        if local:
            loads += [(mask[:, :, :].bitcast(U16), w["mask"]), (maskT[:, :, :].bitcast(U16), w["maskT"])]
        sc.arm(loads)
        with nc.Block() as block:

            @block.vector
            def _(dve):
                nc.vector.memset(V[:, :, :, :], 0.0).then_inc(s_zero, 1)
                nc.vector.memset(mb[:, :, :], 0.0).then_inc(s_zero, 1)
                nc.vector.tensor_copy(KS[96:P, :, :], minus[96:P, :].unsqueeze(2).broadcast_to([32, H, TK]))\
                    .then_inc(s_zero, 1)
                dve.wait_ge(s_zero, 3)
                nc.vector.memset(V[:, :, :, HD:HD + 1], 1.0).then_inc(s_zero, 1)
                if local:
                    nc.vector.memset(xT[:, :, 0:PAD], 0.0).then_inc(s_zero, 1)
                    nc.vector.memset(xT[:, :, PAD + T:TK], 0.0).then_inc(s_zero, 1)
                    nc.vector.memset(KS[0:STACK, :, 0:PAD], 0.0).then_inc(s_zero, 1)
                    nc.vector.memset(KS[0:STACK, :, PAD + T:TK], 0.0).then_inc(s_zero, 1)

        Xp = X[:, :, :].rearrange("p (b j k) d -> p b j (k d)", j=NP2, k=2)
        Xt = X[:, :, :].rearrange("p (b j) d -> p b j d", j=NQ)
        rp, mp = [a[:, :].rearrange("p (b j k) -> p b j k", j=NP2, k=2) for a in (rstd, nmr)]

        def variant(j):
            return 0 if j == 0 else 2 if j == NQ - 1 else 1

        def stack_out(b, c):
            r, h = stacks[c]
            isk, m, tb = steps[r]
            if isk and local:
                return KS[0:STACK, 8 * m + h, PAD + 512 * tb:PAD + 512 * (tb + 1)], 1
            if isk:
                return KS[0:STACK, 4 * h:4 * h + 4, 512 * tb:512 * (tb + 1)], 4
            return QS[0:STACK, 8 * m + h, 512 * tb:512 * (tb + 1)], 1

        def stack_copy(eng, b, c):
            dst, copies = stack_out(b, c)
            src = bs4[2 + c % 2][0:STACK, :]
            if copies > 1:
                src = src.unsqueeze(1).broadcast_to([STACK, copies, 512])
            return eng(dst, src)

        with nc.Block() as block:

            @block.gpsimd
            def _(pool):
                with pool.Fori(0, B) as b:
                    for j in range(NP2):
                        n = NP2 * b + j
                        pool.wait_ge(s_T, freed(n, 2))
                        normalise(pool, nc.gpsimd, sc, by_tile(xl[:, j % 2, :]), by_tile(at(Xp, b, j)), at(rp, b, j),
                                  at(mp, b, j), s_xh, made(n)).then_inc(s_xl, 1)
                        pool.wait_ge(s_xl, made(n))
                        sc.settle(pool)
                        nc.gpsimd.tensor_tensor(by_tile(at(Xp, b, j)), by_tile(at(Xp, b, j)), twice(bo[:, :]),
                                                ALU.add).then_inc(s_xb, 1)

            @block.tensor
            def _(pe):
                def prepare(b):
                    for j in range(NP2):
                        n = NP2 * b + j
                        pe.wait_ge(s_xl, made(n))
                        if j < 2:
                            pe.wait_ge(s_mx, done_before(b, NMX))
                        else:
                            pe.wait_ge(s_xT, freed(n, 2))
                        for i in range(4):
                            ins = nc.tensor.transpose(bk[j % 2][:, i * P:(i + 1) * P], xl[:, j % 2, i * P:(i + 1) * P],
                                                      ident[:, :])
                        ins.then_inc(s_T, 1)
                    c = 0
                    for r in range(R + 1):
                        if r < R:
                            isk, m, tb = steps[r]
                            W, rws = (Wk, KROWS) if isk else (Wq, P)
                            pe.wait_ge(s_xT, made(NP2 * b + 2 * tb + 1))
                            if r < 2:
                                pe.wait_ge(s_e, done_before(b, NU))
                            else:
                                pe.wait_ge(s_f, freed(R * b + r, 2))
                            for ch in range(2):
                                ins = nc.tensor.matmul(bs4[r % 2][0:rws, :], W[:, ch, m * P:m * P + rws],
                                                       xT[:, ch, PAD + 512 * tb:PAD + 512 * (tb + 1)],
                                                       start=(ch == 0), stop=(ch == 1))
                            ins.then_inc(s_fs, 1)
                        while c < len(stacks) and stacks[c][0] < r:
                            rr, h = stacks[c]
                            isk = steps[rr][0]
                            rws = KROWS if isk else P
                            sel = selk if isk else selq
                            pe.wait_ge(s_sp, made(R * b + rr))
                            if c < 2:
                                pe.wait_ge(s_e, done_before(b, NU))
                            pe.wait_ge((s_ka, s_kd)[c % 2], freed(NS2 * b + c // 2, 1))
                            for a in range(3):
                                ins = nc.tensor.matmul(bs4[2 + c % 2][0:STACK, :], sel[0:rws, a, h, :],
                                                       parts[0:rws, rr % 2, a, :], start=(a == 0), stop=(a == 2))
                            ins.then_inc(s_st, 1)
                            c += 1
                    for j in range(NV):
                        n = NV * b + j
                        if j < 2:
                            pe.wait_ge(s_xT, made(NP2 * b + NP2 - 1))
                        else:
                            pe.wait_ge(s_vs, freed(n, 2))
                        for ch in range(2):
                            ins = nc.tensor.matmul(bk[j % 2][:, 0:KVH * HD], xT[:, ch, P * j:P * (j + 1)], Wv[:, ch, :],
                                                   start=(ch == 0), stop=(ch == 1))
                        ins.then_inc(s_v, 1)
                    pe.wait_ge(s_ka, done_before(b, NS2) + NS2)
                    pe.wait_ge(s_kd, done_before(b, NS2) + NS2)
                    pe.wait_ge(s_vs, done_before(b, NV) + NV)

                def max_pass(b, c):
                    n = NMX * b + c
                    pe.wait_ge(s_mx, freed(n, 2))
                    if local:
                        j, hp = c // 8, c % 8
                        nc.tensor.matmul(bk[c % 2][:, :], identb[:, :], mask[:, variant(j), :].unsqueeze(1).broadcast_to([P, 2, 256]), start=True, stop=False,
                                         skip_group_check=True)
                        for k in range(2):
                            ins = nc.tensor.matmul(bk[c % 2][:, 256 * k:256 * (k + 1)],
                                                   QS[0:STACK, 2 * hp + k, P * j:P * (j + 1)],
                                                   KS[0:STACK, 2 * hp + k, P * j:P * (j + 2)], start=False, stop=True,
                                                   skip_group_check=True)
                    else:
                        j, h, e = c // (2 * H), c // 2 % H, c % 2
                        ins = nc.tensor.matmul(bk[e][:, :], QS[0:STACK, h, P * j:P * (j + 1)],
                                               KS[0:STACK, h, 512 * e:512 * (e + 1)], start=True, stop=True)
                    ins.then_inc(s_m, 1)

                def max_transpose(b, j, sums, ys):
                    pe.wait_ge(s_mb, made(NQ * b + j))
                    pe.wait_ge(s_qm, done_before(b, NQ) + j)
                    pe.wait_ge(s_rc, done_before(b, NG) + sums)
                    pe.wait_ge(s_xo, done_before(b, NY) + ys)
                    nc.tensor.transpose(bk[3][:, 0:P // 2].bitcast(BF16), mb[:, j % 2, :], identb[:, :]).then_inc(s_mT, 1)

                def probs(b, c):
                    n = NU * b + c
                    if local:
                        j, hp = c // 8, c % 8
                        if hp == 0:
                            pe.wait_ge(s_qm, made(NQ * b + j))
                        pe.wait_ge(s_e, freed(n, 4))
                        o = bs4[c % 4]
                        nc.tensor.matmul(o, identb[:, :], maskT[:, variant(j), :].unsqueeze(1).broadcast_to([P, 2, 256]), start=True, stop=False,
                                         skip_group_check=True)
                        for k in range(2):
                            for kk in range(2):
                                ins = nc.tensor.matmul(o[:, (2 * k + kk) * P:(2 * k + kk + 1) * P],
                                                       KS[:, 2 * hp + k, P * (j + kk):P * (j + kk + 1)],
                                                       QS[:, 2 * hp + k, P * j:P * (j + 1)], start=False, stop=True,
                                                       skip_group_check=True)
                    else:
                        q, gi, i = c // 64, c % 64 // 4, c % 4
                        g, sp = gi // 4, gi % 4
                        if gi == 0 and i == 0:
                            pe.wait_ge(s_qm, made(NQ * b + 4 * q + 3))
                        pe.wait_ge(s_e, freed(n, 2))
                        for kk in range(2):
                            ins = nc.tensor.matmul(bS[c % 2][:, 512 * kk:512 * (kk + 1)],
                                                   KS[:, 4 * g + i, P * (2 * sp + kk):P * (2 * sp + kk + 1)],
                                                   QS[:, 4 * g + i, 512 * q:512 * (q + 1)], start=True, stop=True)
                    ins.then_inc(s_s, 1)

                def values(b, c):
                    if local:
                        j, g = c // 4, c % 4
                        pe.wait_ge(s_e, made(NU * b + 2 * c + 1))
                        if g == 0:
                            pe.wait_ge(s_os, done_before(b, NG) + j)
                        for kk in range(2):
                            for i in range(4):
                                ins = nc.tensor.matmul(bk[2][32 * i:32 * i + 32, P * g:P * (g + 1)],
                                                       V[:, j + kk, 4 * g + i, :],
                                                       prob[:, c % 2, i, P * kk:P * (kk + 1)],
                                                       start=(kk == 0), stop=(kk == 1), skip_group_check=True)
                    else:
                        q, g, sp = c // 16, c % 16 // 4, c % 4
                        pe.wait_ge(s_e, made(NU * b + 4 * c + 3))
                        if sp == 0:
                            pe.wait_ge(s_os, done_before(b, NG) + 4 * q + g)
                        for kk in range(2):
                            for i in range(4):
                                ins = nc.tensor.matmul(bk[2][32 * i:32 * i + 32, :], V[:, 2 * sp + kk, g, :],
                                                       prob[:, c % 2, i, 512 * kk:512 * (kk + 1)],
                                                       start=(sp == 0 and kk == 0), stop=(sp == 3 and kk == 1),
                                                       skip_group_check=True)
                    ins.then_inc(s_av, 1)

                def sums(b, n, maxes, ys):
                    pe.wait_ge(s_os, made(NG * b + n))
                    pe.wait_ge(s_qm, done_before(b, NQ) + maxes)
                    pe.wait_ge(s_xo, done_before(b, NY) + ys)
                    pe.wait_ge(s_rc, done_before(b, NG) + n)
                    nc.tensor.matmul(bk[3][:, :], sels[:, :], O[:, :], start=True, stop=True).then_inc(s_sum, 1)

                def project(b, n, maxes):
                    gs = n + 1 if local else 4 * (n // 2) + 4
                    pe.wait_ge(s_on, done_before(b, NG) + gs)
                    pe.wait_ge(s_qm, done_before(b, NQ) + maxes)
                    pe.wait_ge(s_xo, done_before(b, NY) + n)
                    for k in range(1 if local else 2):
                        for g in range(4):
                            l = On[:, 0, P * g:P * (g + 1)] if local else On[:, g, P * (2 * (n % 2) + k):P * (2 * (n % 2) + k + 1)]
                            ins = nc.tensor.matmul(bk[3][:, k * D:(k + 1) * D], l, Wo[:, g, :], start=(g == 0),
                                                   stop=(g == 3))
                    ins.then_inc(s_y, 1)

                with pe.Fori(0, B) as b:
                    prepare(b)
                    if local:
                        for c in range(8):
                            max_pass(b, c)
                        max_transpose(b, 0, 0, 0)
                        for j in range(NQ):
                            for hp in range(8):
                                probs(b, 8 * j + hp)
                                if j + 1 < NQ:
                                    max_pass(b, 8 * (j + 1) + hp)
                                if hp % 2 and hp > 1:
                                    values(b, 4 * j + hp // 2 - 1)
                            if j + 1 < NQ:
                                max_transpose(b, j + 1, j, j)
                            values(b, 4 * j + 3)
                            sums(b, j, min(j + 2, NQ), j)
                            project(b, j, min(j + 2, NQ))
                    else:
                        for j in range(4):
                            for c in range(2 * H):
                                max_pass(b, 2 * H * j + c)
                            max_transpose(b, j, 0, 0)
                        for q in range(T // 512):
                            more = q + 1 < T // 512
                            for gi in range(16):
                                mt = min(4 * (q + 1) + gi // 4, NQ) if more else NQ
                                for i in range(4):
                                    probs(b, 64 * q + 4 * gi + i)
                                    if more:
                                        for e in range(2):
                                            max_pass(b, 2 * H * 4 * (q + 1) + 2 * (4 * gi + i) + e)
                                if more and gi % 4 == 3:
                                    max_transpose(b, 4 * (q + 1) + gi // 4, 4 * q + gi // 4, 2 * q)
                                    mt += 1
                                if gi % 4 == 1 and gi > 4:
                                    sums(b, 4 * q + gi // 4 - 1, mt, 2 * q)
                                if gi:
                                    values(b, 16 * q + gi - 1)
                            values(b, 16 * q + 15)
                            sums(b, 4 * q + 3, mt, 2 * q)
                            project(b, 2 * q, mt)
                            project(b, 2 * q + 1, mt)

            @block.scalar
            def _(act):
                def prepare(b):
                    for j in range(NP2):
                        n = NP2 * b + j
                        act.wait_ge(s_T, made(n))
                        act.wait_ge(s_v, done_before(b, NV))
                        nc.scalar.activation(xT[:, :, PAD + 2 * P * j:PAD + 2 * P * (j + 1)].rearrange("p c (k t) -> p k c t", k=2),
                                             bk[j % 2][:, :].rearrange("p (k c t) -> p k c t", k=2, c=2),
                                             ACT.Copy).then_inc(s_xT, 1)
                    c = 0
                    for r in range(R + 1):
                        if r < R:
                            isk, m, tb = steps[r]
                            rws = KROWS if isk else P
                            act.wait_ge(s_fs, made(R * b + r))
                            act.wait_ge(s_sp, freed(R * b + r, 2))
                            nc.scalar.activation(f[0:rws, r % 2, :], bs4[r % 2][0:rws, :], ACT.Identity,
                                                 bias=(kb if isk else qb)[0:rws, m:m + 1]).then_inc(s_f, 1)
                        while c < len(stacks) and stacks[c][0] < r:
                            if c % 2 == 0:
                                act.wait_ge(s_st, made(2 * NS2 * b + c))
                                act.wait_ge(s_s, done_before(b, NU))
                                stack_copy(lambda d, s: nc.scalar.activation(d, s, ACT.Copy), b, c).then_inc(s_ka, 1)
                            c += 1

                def spread_max(b, j):
                    act.wait_ge(s_mT, made(NQ * b + j))
                    nc.scalar.activation(QS[96:P, :, P * j:P * (j + 1)],
                                         bk[3][96:P, 0:P // 2].bitcast(BF16).unsqueeze(1).broadcast_to([32, H, P]),
                                         ACT.Copy).then_inc(s_qm, 1)

                def exps(b, c):
                    act.wait_ge(s_s, made(NU * b + c))
                    if local:
                        act.wait_ge(s_av, made(NAV * b + c // 2 - 2))
                        nc.scalar.activation(prob[:, c // 2 % 2, 2 * (c % 2):2 * (c % 2) + 2, :].rearrange("p i n -> p (i n)"),
                                             bs4[c % 4], ACT.Exp, scale=HD ** -0.5).then_inc(s_e, 1)
                    else:
                        act.wait_ge(s_av, made(NAV * b + c // 4 - 2))
                        nc.scalar.activation(prob[:, c // 4 % 2, c % 4, :], bS[c % 2][:, :], ACT.Exp,
                                             scale=HD ** -0.5).then_inc(s_e, 1)

                def take_sum(b, n):
                    act.wait_ge(s_av, made(NAV * b + 4 * n + 3))
                    act.wait_ge(s_on, done_before(b, NG) + n)
                    act.wait_ge(s_sum, done_before(b, NG) + n)
                    nc.scalar.activation(O[:, :], bk[2][:, :], ACT.Copy).then_inc(s_os, 1)

                with act.Fori(0, B) as b:
                    prepare(b)
                    if local:
                        spread_max(b, 0)
                        for j in range(NQ):
                            for hp in range(8):
                                exps(b, 8 * j + hp)
                            if j + 1 < NQ:
                                spread_max(b, j + 1)
                            take_sum(b, j)
                    else:
                        for j in range(4):
                            spread_max(b, j)
                        for q in range(T // 512):
                            for gi in range(16):
                                for i in range(4):
                                    exps(b, 64 * q + 4 * gi + i)
                                if q + 1 < T // 512 and gi % 4 == 3:
                                    spread_max(b, 4 * (q + 1) + gi // 4)
                                if gi % 4 == 0 and gi:
                                    take_sum(b, 4 * q + gi // 4 - 1)
                            take_sum(b, 4 * q + 3)

            @block.vector
            def _(dve):
                def prepare(b):
                    c = 0
                    for r in range(R + 1):
                        if r < R:
                            isk, m, tb = steps[r]
                            rws = KROWS if isk else P
                            n = R * b + r
                            src, p3 = f[0:rws, r % 2, :], parts[0:rws, r % 2, :, :]
                            dve.wait_ge(s_f, made(n))
                            if r >= 2:
                                first = sum(1 for rr, _ in stacks if rr <= r - 2)
                                dve.wait_ge(s_st, done_before(b, 2 * NS2) + first)
                            nc.vector.tensor_copy(p3[:, 0, :], src).then_inc(s_spq, 1)
                            dve.wait_ge(s_spq, 3 * n + 1 + CREDIT)
                            nc.vector.tensor_tensor(src, src, p3[:, 0, :], ALU.subtract).then_inc(s_spq, 1)
                            dve.wait_ge(s_spq, 3 * n + 2 + CREDIT)
                            nc.vector.tensor_copy(p3[:, 1, :], src).then_inc(s_spq, 1)
                            dve.wait_ge(s_spq, 3 * n + 3 + CREDIT)
                            nc.vector.tensor_tensor(p3[:, 2, :], src, p3[:, 1, :], ALU.subtract).then_inc(s_sp, 1)
                        while c < len(stacks) and stacks[c][0] < r:
                            if c % 2:
                                dve.wait_ge(s_st, made(2 * NS2 * b + c))
                                dve.wait_ge(s_s, done_before(b, NU))
                                stack_copy(nc.vector.tensor_copy, b, c).then_inc(s_kd, 1)
                            c += 1
                    for j in range(NV):
                        n = NV * b + j
                        dve.wait_ge(s_v, made(n))
                        dve.wait_ge(s_av, done_before(b, NAV))
                        nc.vector.tensor_tensor(V[:, j, :, 0:HD], bk[j % 2][:, 0:KVH * HD].rearrange("p (h d) -> p h d", d=HD),
                                                bv[:, :].rearrange("p (h d) -> p h d", d=HD), ALU.add).then_inc(s_vs, 1)

                def maxima(b, c):
                    n = NMX * b + c
                    dve.wait_ge(s_m, made(n))
                    if local:
                        j, hp = c // 8, c % 8
                        if hp == 0:
                            dve.wait_ge(s_mb, freed(NQ * b + j, 2))
                        nc.vector.tensor_reduce(m1[:, j % 2, 2 * hp:2 * hp + 2], by_tile(bk[c % 2][:, :]), AX,
                                                ALU.max).then_inc(s_mx, 1)
                    else:
                        j, h, e = c // (2 * H), c // 2 % H, c % 2
                        if c % (2 * H) == 0:
                            dve.wait_ge(s_m1, freed(NQ * b + j, 2))
                        nc.vector.tensor_reduce(mx[:, j % 2, h, e:e + 1], bk[e][:, :], AX, ALU.max).then_inc(s_mx, 1)

                def split_max(b, j):
                    n = NQ * b + j
                    dve.wait_ge(s_mx, done_before(b, NMX) + (j + 1) * NMX // NQ)
                    if not local:
                        dve.wait_ge(s_mb, freed(n, 2))
                        nc.vector.tensor_tensor(m1[:, j % 2, :], mx[:, j % 2, :, 0], mx[:, j % 2, :, 1],
                                                ALU.max).then_inc(s_m1, 1)
                        dve.wait_ge(s_m1, made(n))
                    dve.wait_ge(s_mT, freed(n, 2))
                    nc.vector.tensor_copy(mb[:, j % 2, 96:112], m1[:, j % 2, :]).then_inc(s_mh, 1)
                    dve.wait_ge(s_mh, made(n))
                    nc.vector.tensor_tensor(mb[:, j % 2, 112:128], m1[:, j % 2, :], mb[:, j % 2, 96:112],
                                            ALU.subtract).then_inc(s_mb, 1)

                def normalise(b, n):
                    dve.wait_ge(s_sum, made(NG * b + n))
                    nc.vector.reciprocal(Rc, bk[3][:, :]).then_inc(s_rc, 1)
                    dve.wait_ge(s_rc, made(NG * b + n))
                    dve.wait_ge(s_y, done_before(b, NY) + (n if local else 2 * (n // 4)))
                    nc.vector.tensor_tensor(On[:, 0 if local else n % 4, :], O, Rc, ALU.mult).then_inc(s_on, 1)

                def add_out(b, n):
                    dve.wait_ge(s_y, made(NY * b + n))
                    dve.wait_ge(s_xb, done_before(b, NP2) + NP2)
                    if local:
                        nc.vector.tensor_tensor(at(Xt, b, n), at(Xt, b, n), bk[3][:, 0:D], ALU.add).then_inc(s_xo, 1)
                    else:
                        nc.vector.tensor_tensor(at(Xp, b, n), at(Xp, b, n), bk[3][:, :], ALU.add).then_inc(s_xo, 1)

                with dve.Fori(0, B) as b:
                    prepare(b)
                    if local:
                        for c in range(8):
                            maxima(b, c)
                        split_max(b, 0)
                        for j in range(NQ):
                            if j + 1 < NQ:
                                for hp in range(8):
                                    maxima(b, 8 * (j + 1) + hp)
                                split_max(b, j + 1)
                            normalise(b, j)
                            add_out(b, j)
                    else:
                        for j in range(4):
                            for c in range(2 * H):
                                maxima(b, 2 * H * j + c)
                            split_max(b, j)
                        for q in range(T // 512):
                            more = q + 1 < T // 512
                            for gi in range(16):
                                if more:
                                    for c in range(8):
                                        maxima(b, 2 * H * 4 * (q + 1) + 8 * gi + c)
                                    if gi % 4 == 3:
                                        split_max(b, 4 * (q + 1) + gi // 4)
                                if gi % 4 == 1 and gi > 4:
                                    normalise(b, 4 * q + gi // 4 - 1)
                            normalise(b, 4 * q + 3)
                            add_out(b, 2 * q)
                            add_out(b, 2 * q + 1)


LANES = 4
SPLIT = 4097.0


class Count:

    def __init__(self, start):
        self.start, self.n = start, 0

    def made(self):
        return self.start + self.n

    def one(self):
        self.n += 1
        return 1


def exact_alpha(nc, X, NT, name, w, za):
    GT = min(16, NT)
    GP = NT // GT
    VAR_STEPS = 9
    STAT_STEPS, HEAD_STEPS, SUM_STEPS, KS = 49, 9, 8, D // LANES
    with Scope(nc, name) as sc:
        big = sc.sb("big", [P, 8 * GT, D])
        on32 = sc.sb("on32", [P, D])
        Wa, Wh, Wl = [sc.sb(n, [P, 2, D]) for n in ("Wa", "Wh", "Wl")]
        mean = sc.sb("mean", [P, NT, 1])
        acc, su, bb, er, dd = [sc.sb(n, [P, 1, 2 * GT, LANES]) for n in ("acc", "su", "bb", "er", "dd")]
        z2 = sc.sb("z2", [P, 2 * GT, 2])
        var, root, rinv, rh, rl, ra, rb = [sc.sb(n, [P, GT]) for n in ("var", "root", "rinv", "rh", "rl", "ra", "rb")]
        s_w = sc.sem("w")
        s_m = sc.sem("m")
        s_d = sc.sem("d")
        s_r = sc.sem("root")
        s_0 = sc.sem("h0")
        s_1 = sc.sem("h1")
        s_c = sc.sem("c")
        s_z = sc.sem("z")
        ph = big[:, 0:2 * GT, :]
        pl = big[:, 2 * GT:4 * GT, :]
        cen, aux, hi, lo = [big[:, (4 + i) * GT:(5 + i) * GT, :] for i in range(4)]
        q = ph[:, 0:GT, :]
        sc.arm([(on32[:, :], spread(w["on32"])), (Wa[:, :, :], spread(w["walpha"]))])

        SHARE = GT * 5 // 8

        def head(a, h, tiles):
            return a[:, h:h + 1, :].broadcast_to([P, tiles.stop - tiles.start, D])

        def per_tile(a):
            return a[:, :].unsqueeze(2).broadcast_to([P, GT, D])

        def group(a, g):
            return a[:, :, :].rearrange("p (g t) d -> p g t d", t=GT)[:, bass.ds(g, 1), :, :]

        def low_products(eng, tt, sem, m, h, tiles, spare):
            low, rounded = [a[:, h * GT + tiles.start:h * GT + tiles.stop, :] for a in (pl, ph)]
            hi_, lo_, spare = hi[:, tiles, :], lo[:, tiles, :], spare[:, tiles, :]
            tt(low, hi_, head(Wh, h, tiles), ALU.mult).then_inc(sem, m.one())
            eng.wait_ge(sem, m.made())
            tt(low, low, rounded, ALU.subtract).then_inc(sem, m.one())
            for a, b in ((hi_, Wl), (lo_, Wh), (lo_, Wl)):
                tt(spare, a, head(b, h, tiles), ALU.mult).then_inc(sem, m.one())
                eng.wait_ge(sem, m.made())
                tt(low, low, spare, ALU.add).then_inc(sem, m.one())
                eng.wait_ge(sem, m.made())

        with nc.Block() as block:

            @block.scalar
            def _(act):
                with act.Fori(0, GP) as g:
                    act.wait_ge(s_d, STAT_STEPS * g + CREDIT + VAR_STEPS)
                    nc.scalar.activation(root[:, :], var[:, :], ACT.Ln).then_inc(s_r, 1)
                    act.wait_ge(s_r, made(2 * g))
                    nc.scalar.activation(root[:, :], root[:, :], ACT.Exp, scale=0.5).then_inc(s_r, 1)

            @block.gpsimd
            def _(pool):
                with pool.Fori(0, GP) as g:
                    m = Count(HEAD_STEPS * g + CREDIT)
                    pool.wait_ge(s_d, STAT_STEPS * g + STAT_STEPS + CREDIT)
                    tiles = slice(0, SHARE)
                    nc.gpsimd.tensor_tensor(ph[:, GT:GT + SHARE, :], q[:, tiles, :], head(Wa, 1, tiles),
                                            ALU.mult).then_inc(s_1, m.one())
                    pool.wait_ge(s_1, m.made())
                    low_products(pool, nc.gpsimd.tensor_tensor, s_1, m, 1, tiles, aux)
                    assert m.n == HEAD_STEPS

            @block.vector
            def _(dve):
                tt = nc.vector.tensor_tensor
                ts = nc.vector.tensor_scalar

                def halves(sem, n, a, upper, lower, spare):
                    ts(spare, a, SPLIT, None, ALU.mult).then_inc(sem, n.one())
                    dve.wait_ge(sem, n.made())
                    tt(upper, spare, a, ALU.subtract).then_inc(sem, n.one())
                    dve.wait_ge(sem, n.made())
                    tt(upper, spare, upper, ALU.subtract).then_inc(sem, n.one())
                    dve.wait_ge(sem, n.made())
                    tt(lower, a, upper, ALU.subtract).then_inc(sem, n.one())
                    dve.wait_ge(sem, n.made())

                def less_products(sem, n, a, pairs, spare):
                    for x, y in pairs:
                        tt(spare, x, y, ALU.mult).then_inc(sem, n.one())
                        dve.wait_ge(sem, n.made())
                        tt(a, a, spare, ALU.subtract).then_inc(sem, n.one())
                        dve.wait_ge(sem, n.made())

                n = Count(CREDIT)
                halves(s_w, n, Wa[:, :, :], Wh[:, :, :], Wl[:, :, :], Wl[:, :, :])
                n = Count(CREDIT)
                flat8 = big[:, 0:4, :].rearrange("p a b -> p (a b)")
                lanes = flat8[:, 0:NT * 16].rearrange("p (t l) -> p t l", l=16)
                m8 = big[:, 4:6, :].rearrange("p a b -> p (a b)")[:, 0:NT * 8].rearrange("p (t l) -> p t l", l=8)
                tt(lanes, X[:, 0:NT, 0:16], X[:, 0:NT, 16:32], ALU.add).then_inc(s_m, n.one())
                for k in range(2, 16):
                    dve.wait_ge(s_m, n.made())
                    tt(lanes, lanes, X[:, 0:NT, 16 * k:16 * k + 16], ALU.add).then_inc(s_m, n.one())
                dve.wait_ge(s_m, n.made())
                tt(m8[:, :, 0:4], lanes[:, :, 0:4], lanes[:, :, 4:8], ALU.add).then_inc(s_m, n.one())
                tt(m8[:, :, 4:8], lanes[:, :, 8:12], lanes[:, :, 12:16], ALU.add).then_inc(s_m, n.one())
                dve.wait_ge(s_m, n.made())
                tt(lanes[:, :, 0:4], m8[:, :, 0:4], m8[:, :, 4:8], ALU.add).then_inc(s_m, n.one())
                dve.wait_ge(s_m, n.made())
                tt(m8[:, :, 0:2], lanes[:, :, 0:4:2], lanes[:, :, 1:4:2], ALU.add).then_inc(s_m, n.one())
                dve.wait_ge(s_m, n.made())
                tt(mean[:, :, :], m8[:, :, 0:1], m8[:, :, 1:2], ALU.add).then_inc(s_m, n.one())
                dve.wait_ge(s_m, n.made())
                ts(mean[:, :, :], mean[:, :, :], 1.0 / D, None, ALU.mult).then_inc(s_m, n.one())
                dve.wait_ge(s_m, n.made())
                with dve.Fori(0, GP) as g:
                    n = Count(STAT_STEPS * g + CREDIT)
                    tt(cen.unsqueeze(1), group(X, g), group(mean, g).broadcast_to([P, 1, GT, D]),
                       ALU.subtract).then_inc(s_d, n.one())
                    dve.wait_ge(s_d, n.made())
                    tt(hi, cen, cen, ALU.mult).then_inc(s_d, n.one())
                    nc.vector.tensor_copy(aux, on32[:, :].unsqueeze(1).broadcast_to([P, GT, D])).then_inc(s_d, n.one())
                    dve.wait_ge(s_d, n.made())
                    nc.vector.tensor_tensor_scan(flat(lo), flat(aux), flat(hi), 0.0, ALU.mult,
                                                 ALU.add).then_inc(s_d, n.one())
                    dve.wait_ge(s_d, n.made())
                    window = lo[:, :, 31:D:32]
                    tt(hi[:, :, 0:4], window[:, :, 0:4], window[:, :, 4:8], ALU.add).then_inc(s_d, n.one())
                    dve.wait_ge(s_d, n.made())
                    tt(hi[:, :, 4:6], hi[:, :, 0:4:2], hi[:, :, 1:4:2], ALU.add).then_inc(s_d, n.one())
                    dve.wait_ge(s_d, n.made())
                    tt(hi[:, :, 6], hi[:, :, 4], hi[:, :, 5], ALU.add).then_inc(s_d, n.one())
                    dve.wait_ge(s_d, n.made())
                    ts(var[:, :], hi[:, :, 6], 1.0 / D, None, ALU.mult).then_inc(s_d, n.one())
                    dve.wait_ge(s_d, n.made())
                    ts(var[:, :], var[:, :], 1e-5, None, ALU.add).then_inc(s_d, n.one())
                    assert n.n == VAR_STEPS
                    dve.wait_ge(s_r, 2 * g + 2 + CREDIT)
                    nc.vector.reciprocal(rinv[:, :], root[:, :]).then_inc(s_d, n.one())
                    halves(s_d, n, root[:, :], rh[:, :], rl[:, :], ra[:, :])
                    less_products(s_d, n, var[:, :], ((rh[:, :], rh[:, :]), (rh[:, :], rl[:, :]), (rl[:, :], rh[:, :]),
                                                      (rl[:, :], rl[:, :])), ra[:, :])
                    tt(rb[:, :], var[:, :], rinv[:, :], ALU.mult).then_inc(s_d, n.one())
                    dve.wait_ge(s_d, n.made())
                    ts(rb[:, :], rb[:, :], 0.5, None, ALU.mult).then_inc(s_d, n.one())
                    dve.wait_ge(s_d, n.made())
                    tt(root[:, :], root[:, :], rb[:, :], ALU.add).then_inc(s_d, n.one())
                    dve.wait_ge(s_d, n.made())
                    nc.vector.reciprocal(rinv[:, :], root[:, :]).then_inc(s_d, n.one())
                    halves(s_d, n, root[:, :], rh[:, :], rl[:, :], ra[:, :])
                    tt(q, cen, per_tile(rinv), ALU.mult).then_inc(s_d, n.one())
                    dve.wait_ge(s_d, n.made())
                    halves(s_d, n, q, hi, lo, aux)
                    less_products(s_d, n, cen, ((hi, per_tile(rh)), (hi, per_tile(rl)), (lo, per_tile(rh)),
                                                (lo, per_tile(rl))), aux)
                    tt(cen, cen, per_tile(rinv), ALU.mult).then_inc(s_d, n.one())
                    dve.wait_ge(s_d, n.made())
                    tt(q, q, cen, ALU.add).then_inc(s_d, n.one())
                    dve.wait_ge(s_d, n.made())
                    halves(s_d, n, q, hi, lo, aux)
                    assert n.n == STAT_STEPS, n.n
                    m = Count(2 * HEAD_STEPS * g + CREDIT)
                    tiles, rest = slice(0, GT), slice(SHARE, GT)
                    tt(ph[:, GT + SHARE:2 * GT, :], q[:, rest, :], head(Wa, 1, rest), ALU.mult).then_inc(s_0, m.one())
                    dve.wait_ge(s_0, m.made())
                    low_products(dve, tt, s_0, m, 1, rest, cen)
                    dve.wait_ge(s_1, HEAD_STEPS * g + CREDIT + 1)
                    tt(q, q, head(Wa, 0, tiles), ALU.mult).then_inc(s_0, m.one())
                    dve.wait_ge(s_0, m.made())
                    low_products(dve, tt, s_0, m, 0, tiles, cen)
                    z = Count(4 * g + CREDIT)
                    nc.vector.memset(acc[:, :, :, :], 0.0).then_inc(s_z, z.one())
                    dve.wait_ge(s_z, z.made())
                    dve.wait_ge(s_1, HEAD_STEPS * g + HEAD_STEPS + CREDIT)
                    sc.settle(dve)
                    with dve.Fori(0, KS) as k:
                        c = Count(SUM_STEPS * KS * g + SUM_STEPS * k + CREDIT)
                        high, low = [a.rearrange("p t (k l) -> p k t l", l=LANES)[:, bass.ds(k, 1), :, :]
                                     for a in (ph, pl)]
                        a_, s_, b_, e_, d_ = [b[:, :, :, :] for b in (acc, su, bb, er, dd)]
                        dve.wait_ge(s_c, c.made())
                        tt(s_, a_, high, ALU.add).then_inc(s_c, c.one())
                        dve.wait_ge(s_c, c.made())
                        tt(b_, s_, a_, ALU.subtract).then_inc(s_c, c.one())
                        dve.wait_ge(s_c, c.made())
                        tt(e_, s_, b_, ALU.subtract).then_inc(s_c, c.one())
                        tt(d_, high, b_, ALU.subtract).then_inc(s_c, c.one())
                        dve.wait_ge(s_c, c.made())
                        tt(e_, a_, e_, ALU.subtract).then_inc(s_c, c.one())
                        dve.wait_ge(s_c, c.made())
                        tt(e_, e_, d_, ALU.add).then_inc(s_c, c.one())
                        dve.wait_ge(s_c, c.made())
                        tt(e_, e_, low, ALU.add).then_inc(s_c, c.one())
                        dve.wait_ge(s_c, c.made())
                        tt(a_, s_, e_, ALU.add).then_inc(s_c, c.one())
                        assert c.n == SUM_STEPS
                    dve.wait_ge(s_c, SUM_STEPS * KS * g + SUM_STEPS * KS + CREDIT)
                    tt(z2[:, :, :], acc[:, 0, :, 0:LANES:2], acc[:, 0, :, 1:LANES:2], ALU.add).then_inc(s_z, z.one())
                    dve.wait_ge(s_z, z.made())
                    for h in range(2):
                        tt(group(za, g)[:, :, :, h], z2[:, h * GT:(h + 1) * GT, 0].unsqueeze(1),
                           z2[:, h * GT:(h + 1) * GT, 1].unsqueeze(1), ALU.add).then_inc(s_z, z.one())
                    dve.wait_ge(s_z, z.made())


EXP_C = (0.00019875691214110702, 0.001398199936375022, 0.008333452045917511, 0.04166579619050026, 0.1666666567325592)
LOG1P_D = (15.062909126281738, 83.04756927490234, 221.7624053955078, 309.0987243652344, 216.42788696289062,
           60.11865997314453)
LOG1P_N = (4.527000055531971e-05, 0.4985410273075104, 6.578732490539551, 29.91191864013672, 60.949668884277344,
           57.11296463012695, 20.039552688598633)
LOG_C = ((0.07037683576345444, -0.11514610052108765, 0.11676998436450958),
         (-0.12420140951871872, 0.14249323308467865, -0.16668057441711426),
         (0.2000071406364441, -0.24999994039535522, 0.3333333134651184))
LN2_HIGH, LN2_LOW = 0.693359375, -0.00021219444170128554
ROUNDER = 1.5 * 2 ** 23


def exact_decay(nc, NT, name, w, za, ld):
    N2 = NT * 2
    N = N2 + 2
    with Scope(nc, name) as sc:
        dtb = sc.sb("dtb", [P, 2])
        x, y, n, r, p, e, q = [sc.sb(k, [P, N]) for k in ("x", "y", "n", "r", "p", "e", "q")]
        z, e2, e3, num, den, t, t3, a, b, s, small = [sc.sb(k, [P, N2]) for k in (
            "z", "e2", "e3", "num", "den", "t", "t3", "a", "b", "s", "small")]
        power = sc.sb("power", [P, N], mybir.dt.int32)
        s_s = sc.sem("s")
        sc.arm([(dtb[:, :], spread(w["dtb"])), (x[:, N2:N], spread(w["alog"]))])
        with nc.Block() as block:

            @block.vector
            def _(dve):
                k = Count(CREDIT)

                def tt(out, in0, in1, op):
                    nc.vector.tensor_tensor(out, in0, in1, op).then_inc(s_s, k.one())
                    dve.wait_ge(s_s, k.made())

                def ts(out, in0, c0, c1, *ops):
                    nc.vector.tensor_scalar(out, in0, c0, c1, *ops).then_inc(s_s, k.one())
                    dve.wait_ge(s_s, k.made())

                def stt(out, in0, c, in1, op0, op1):
                    nc.vector.scalar_tensor_tensor(out=out, in0=in0, scalar=c, in1=in1, op0=op0,
                                                   op1=op1).then_inc(s_s, k.one())
                    dve.wait_ge(s_s, k.made())

                X_, Y, NN, R, PP, E, Q = [v[:, :] for v in (x, y, n, r, p, e, q)]
                tt(z[:, :].rearrange("p (t h) -> p t h", h=2), za[:, :, :],
                   dtb[:, :].unsqueeze(1).broadcast_to([P, NT, 2]), ALU.add)
                stt(x[:, 0:N2], z[:, :], -1.0, z[:, :], ALU.mult, ALU.min)
                ts(X_, X_, -87.80000305175781, 88.80000305175781, ALU.max, ALU.min)
                ts(Y, X_, 1.4426950216293335, 0.5, ALU.mult, ALU.add)
                ts(NN, Y, ROUNDER, -ROUNDER, ALU.add, ALU.add)
                tt(Q, NN, Y, ALU.is_gt)
                tt(NN, NN, Q, ALU.subtract)
                ts(NN, NN, -127.0, 127.0, ALU.max, ALU.min)
                ts(power[:, :], NN, 127.0, 2.0 ** 23, ALU.add, ALU.mult)
                stt(R, NN, -LN2_HIGH, X_, ALU.mult, ALU.add)
                stt(R, NN, -LN2_LOW, R, ALU.mult, ALU.add)
                ts(PP, R, EXP_C[0], None, ALU.mult)
                for c in EXP_C[1:]:
                    stt(PP, PP, c, R, ALU.add, ALU.mult)
                tt(Q, R, R, ALU.mult)
                stt(PP, PP, 0.5, Q, ALU.add, ALU.mult)
                tt(PP, PP, R, ALU.add)
                stt(E, PP, 1.0, power[:, :].bitcast(F32), ALU.add, ALU.mult)
                V = e[:, 0:N2]
                E2, E3, NU, DE, TT, T3, A, B, S, SM, Z = [v[:, :] for v in (e2, e3, num, den, t, t3, a, b, s, small, z)]
                tt(E2, V, V, ALU.mult)
                tt(E3, V, E2, ALU.mult)
                stt(DE, V, LOG1P_D[0], V, ALU.add, ALU.mult)
                for c in LOG1P_D[1:-1]:
                    stt(DE, DE, c, V, ALU.add, ALU.mult)
                ts(DE, DE, LOG1P_D[-1], None, ALU.add)
                ts(NU, V, LOG1P_N[0], None, ALU.mult)
                for c in LOG1P_N[1:-1]:
                    stt(NU, NU, c, V, ALU.add, ALU.mult)
                ts(NU, NU, LOG1P_N[-1], None, ALU.add)
                nc.vector.reciprocal(DE, DE).then_inc(s_s, k.one())
                dve.wait_ge(s_s, k.made())
                tt(NU, NU, DE, ALU.mult)
                tt(E3, E3, NU, ALU.mult)
                stt(S, E2, -0.5, E3, ALU.mult, ALU.add)
                tt(S, S, V, ALU.add)
                ts(TT, V, 1.0, None, ALU.add)
                ts(TT, TT, 0.5, -1.0, ALU.mult, ALU.add)
                tt(E2, TT, TT, ALU.mult)
                tt(T3, E2, TT, ALU.mult)
                for out, (c0, c1, c2) in ((A, LOG_C[0]), (B, LOG_C[1]), (NU, LOG_C[2])):
                    ts(out, TT, c0, c1, ALU.mult, ALU.add)
                    tt(out, out, TT, ALU.mult)
                    ts(out, out, c2, None, ALU.add)
                tt(A, A, T3, ALU.mult)
                tt(A, A, B, ALU.add)
                tt(A, A, T3, ALU.mult)
                tt(A, A, NU, ALU.add)
                tt(A, A, T3, ALU.mult)
                ts(A, A, LN2_LOW, None, ALU.add)
                stt(TT, E2, -0.5, TT, ALU.mult, ALU.add)
                tt(TT, TT, A, ALU.add)
                ts(TT, TT, LN2_HIGH, None, ALU.add)
                ts(SM, V, 0.4142135679721832, None, ALU.is_lt)
                tt(S, S, SM, ALU.mult)
                ts(SM, SM, -1.0, 1.0, ALU.mult, ALU.add)
                tt(TT, TT, SM, ALU.mult)
                tt(S, S, TT, ALU.add)
                stt(S, Z, 0.0, S, ALU.max, ALU.add)
                stt(ld[:, :, :], s[:, :].rearrange("p (t h) -> p t h", h=2), -1.0,
                    e[:, N2:N].unsqueeze(1).broadcast_to([P, NT, 2]), ALU.mult, ALU.mult)


CHUNK = 64
DK = 128


def delta_rule(nc, X, B, T, name, w, ident, eps):
    NT = B * T // P
    NB = T // P
    N2 = NT * 2
    LEVELS = 5
    with Scope(nc, name + "g") as gates, Scope(nc, name) as sc:
        za = gates.sb("za", [P, NT, 2])
        ld = gates.sb("ld", [P, NT, 2])
        exact_alpha(nc, X, NT, name + "a", w, za)
        exact_decay(nc, NT, name + "d", w, za, ld)
        Ww = sc.sb("Ww", [P, 2, D])
        Wr = sc.sb("Wr", [P, 2, D])
        Wab = sc.sb("Wab", [P, 2, 4])
        on16 = sc.sb("on16", [P, P])
        on4 = sc.sb("on4", [P, 8])
        ldT = sc.sb("ldT", [P, P])
        inner = sc.sb("inner", [P, P])
        sums = sc.sb("sums", [P, 8])
        pre = sc.sb("pre", [P, 8])
        cumT = sc.sb("cumT", [P, P])
        gapT = sc.sb("gapT", [P, P])
        msk = sc.sb("msk", [P, P])
        flag = sc.sb("flag", [P, NT])
        c25 = sc.sb("c25", [P, 2])
        rstd = sc.sb("rstd", [P, NT])
        nmr = sc.sb("nmr", [P, NT])
        xl = sc.sb("xl", [P, 2, D])
        xT = sc.sb("xT", [P, 2 * P])
        sq = sc.sb("sq", [P, 2, P])
        ss2 = sc.sb("ss2", [P, 2, 2])
        ga = sc.sb("ga", [P, NT, 4])
        ssa = sc.sb("ssa", [P, NT, 2])
        zb, beta, nbeta, cum, dec, tail, bd, rn, w2 = [sc.sb(n, [P, NT, 2]) for n in (
            "zb", "beta", "nbeta", "cum", "dec", "tail", "bd", "rn", "w2")]
        rk = sc.sb("rk", [P, D])
        rkx = sc.sb("rkx", [P, 2, 1 + P])
        cumt = sc.sb("cumt", [P, 2])
        cr = sc.sb("cr", [P, 2, P])
        drow = sc.sb("drow", [P, 2, 2, P])
        tmp = sc.sb("gap", [P, 2, P])
        L = sc.sb("L", [P, 2, P])
        Mi = sc.sb("Mi", [P, 4, P])
        PP = sc.sb("PP", [P, 2, 2, 2, P])
        AT = sc.sb("AT", [P, 2, 2, P])
        iT = sc.sb("iT", [P, 2, 2, P])
        vsc = sc.sb("vsc", [P, 2, P])
        wkd = sc.sb("wkd", [P, 2, P])
        wkt = sc.sb("wkt", [P, 2, 2, P])
        UW = sc.sb("UW", [P, 2, 4 * P])
        rkd = sc.sb("rkd", [P, 2, 2, P])
        xr = sc.sb("xr", [P, 2, D])
        S = sc.sb("S", [P, 2, P])
        vn = sc.sb("vn", [P, 2, P])
        oT = sc.sb("oT", [P, 2, P])
        bk = [sc.ps(f"bk{i}", [P, 4, P]) for i in range(8)]
        s_ain, s_aT, s_axT, s_asq, s_ag, s_agc, s_asc = [sc.sem("a" + n) for n in (
            "in", "T", "xT", "sq", "g", "gc", "sc")]
        (s_xl, s_rk, s_xr, s_cumt, s_T, s_c0, s_xT, s_rkx, s_vw, s_gr, s_crp, s_cr, s_dr, s_vs, s_wkd, s_wkt, s_tmp,
         s_L, s_M, s_in, s_MI, s_MT, s_iT, s_A0, s_sqp, s_PP, s_atp, s_AT, s_uwp, s_UW, s_rkd, s_S0, s_ws, s_vn,
         s_o, s_ds, s_S, s_oT, s_y, s_x) = [sc.sem(n) for n in (
             "xl", "rk", "xr", "cumt", "T", "c0", "xT", "rkx", "vw", "gr", "crp", "cr", "dr", "vs", "wkd", "wkt",
             "tmp", "L", "M", "in", "MI", "MT", "iT", "A0", "sqp", "PP", "atp", "AT", "uwp", "UW", "rkd", "S0",
             "ws", "vn", "o", "ds", "S", "oT", "y", "x")]
        s_ah = sc.sem("ah")
        s_xh = sc.sem("xh")
        s_z = sc.plain_sem("z")
        s_gd = sc.plain_sem("gd")
        s_ga = sc.plain_sem("ga")
        s_gp = sc.plain_sem("gp")
        with nc.Block() as block:

            @block.vector
            def _(dve):
                nc.vector.memset(S[:, :, :], 0.0).then_inc(s_z, 1)
                nc.vector.memset(pre[:, :], 0.0).then_inc(s_z, 1)
                nc.vector.memset(rkx[:, :, :], 0.0).then_inc(s_z, 1)
                nc.vector.memset(c25[:, 0:1], 25 * float(np.log(2.0))).then_inc(s_z, 1)
                nc.vector.memset(c25[:, 1:2], 1.0).then_inc(s_z, 1)

        sc.arm([(Ww[:, :, :], rows(w["wwT"])), (Wr[:, :, :], rows(w["wrT"])), (Wab[:, :, :], rows(w["wab"])),
                (on16[:, :], spread(w["on16"])), (on4[:, :], spread(w["on4"])), (msk[:, :], w["msk"]),
                (flag[:, :], spread(w["flag"][0:NT]))])
        norm_stats(nc, X, NT, rstd, nmr, sc, eps)
        Xv = X[:, :, :].rearrange("p (g v) d -> p g v d", v=2)

        def col(a, g, v, h=None):
            c = a[:, :, :].rearrange("p (g v) h -> p g v h", v=2)[:, bass.ds(g, 1), v, :]
            return flat_h(c) if h is None else flat_h(c)[:, h:h + 1]

        def flat_h(c):
            return c.rearrange("p a h -> p (a h)")

        def col1(a, g, v):
            return a[:, :].rearrange("p (g v) -> p g v", v=2)[:, bass.ds(g, 1), v]

        def wide(c):
            return c.unsqueeze(2).broadcast_to([P, 2, P])

        with nc.Block() as block:

            @block.gpsimd
            def _(pool):
                with pool.Fori(0, NT // 2) as g:
                    for v in range(2):
                        t = 2 * g + v
                        pool.wait_ge(s_aT, freed(t, 2))
                        pool.wait_ge(s_asq, freed(t, 2))
                        normalise(pool, nc.gpsimd, sc, xl[:, v:v + 1, :], Xv[:, bass.ds(g, 1), v, :], col1(rstd, g, v),
                                  col1(nmr, g, v), s_ah, made(t)).then_inc(s_ain, 1)

            @block.tensor
            def _(pe):
                with pe.Fori(0, NT // 2) as g:
                    for v in range(2):
                        t = 2 * g + v
                        pe.wait_ge(s_ain, made(t))
                        pe.wait_ge(s_axT, freed(t, 2))
                        for c in range(2):
                            i = nc.tensor.transpose(bk[v][:, c, :], xl[:, v, c * P:(c + 1) * P], ident[:, :])
                        i.then_inc(s_aT, 1)
                        pe.wait_ge(s_axT, made(t))
                        pe.wait_ge(s_agc, freed(t, 2))
                        for c in range(2):
                            i = nc.tensor.matmul(bk[2 + v][:, 0, 0:4], xT[:, c * P:(c + 1) * P], Wab[:, c, :],
                                                 start=(c == 0), stop=(c == 1))
                        i.then_inc(s_ag, 1)
                nc.tensor.transpose(bk[4][0:N2, 0, :], ld[:, :, :].rearrange("p t h -> p (t h)"),
                                    ident[:, :]).then_inc(s_gp, 1)
                pe.wait_ge(s_gd, 7)
                nc.tensor.transpose(bk[4][:, 0, 0:N2], cumT[0:N2, :], ident[0:N2, 0:N2])
                nc.tensor.transpose(bk[4][:, 1, 0:N2], gapT[0:N2, :], ident[0:N2, 0:N2]).then_inc(s_gp, 1)

            @block.scalar
            def _(act):
                with act.Fori(0, NT // 2) as g:
                    for v in range(2):
                        t = 2 * g + v
                        act.wait_ge(s_ain, made(t))
                        act.wait_ge(s_asc, freed(t, 2))
                        if v == 0:
                            act.wait_ge(s_asq, freed(t, 1))
                        for h in range(2):
                            i = nc.scalar.activation(sq[:, h, :], xl[:, v, h * P:(h + 1) * P], ACT.Square,
                                                     accum_out=ss2[:, v, h:h + 1])
                            if h == 1:
                                i.then_inc(s_asq, 1)
                        act.wait_ge(s_aT, made(t))
                        act.wait_ge(s_ag, freed(t, 1))
                        nc.scalar.activation(xT[:, :], bk[v][:, 0:2, :].rearrange("p a b -> p (a b)"),
                                             ACT.Copy).then_inc(s_axT, 1)
                        if v == 0:
                            act.wait_ge(s_asq, made(t))
                act.wait_ge(s_gd, 1)
                nc.scalar.activation(zb[:, :, :], ga[:, :, 2:4], ACT.Exp, scale=-1.0).then_inc(s_ga, 1)
                nc.scalar.activation(rn[:, :, :], rn[:, :, :], ACT.Ln).then_inc(s_ga, 1)
                act.wait_ge(s_ga, 2)
                nc.scalar.activation(rn[:, :, :], rn[:, :, :], ACT.Exp, scale=-0.5, bias=c25[:, 0:1]).then_inc(s_ga, 1)
                act.wait_ge(s_gd, 9)
                nc.scalar.activation(dec[:, :, :], cum[:, :, :], ACT.Exp).then_inc(s_ga, 1)
                nc.scalar.activation(tail[:, :, :], w2[:, :, :], ACT.Exp).then_inc(s_ga, 1)

            @block.vector
            def _(dve):
                with dve.Fori(0, NT // 2) as g:
                    for v in range(2):
                        t = 2 * g + v
                        dve.wait_ge(s_ag, made(t))
                        nc.vector.tensor_copy(tile_of(ga[:, :, :].rearrange("p (g v) h -> p g v h", v=2), g, v),
                                              bk[2 + v][:, 0, 0:4]).then_inc(s_agc, 1)
                        dve.wait_ge(s_asq, made(t))
                        nc.vector.tensor_copy(col(ssa, g, v), ss2[:, v, :]).then_inc(s_asc, 1)
                dve.wait_ge(s_agc, NT + CREDIT)
                dve.wait_ge(s_asc, NT + CREDIT)
                nc.vector.tensor_scalar(rn[:, :, :], ssa[:, :, :], 1e-24, 2.0 ** 50, ALU.max, ALU.mult).then_inc(s_gd, 1)
                dve.wait_ge(s_gp, 1)
                nc.vector.tensor_copy(ldT[0:N2, :], bk[4][0:N2, 0, :]).then_inc(s_gd, 1)
                dve.wait_ge(s_gd, 2)
                nc.vector.tensor_tensor_scan(inner[0:N2, :], on16[0:N2, :], ldT[0:N2, :], 0.0, ALU.mult,
                                             ALU.add).then_inc(s_gd, 1)
                dve.wait_ge(s_gd, 3)
                nc.vector.tensor_tensor_scan(sums[0:N2, :], on4[0:N2, :], inner[0:N2, 15:P:16], 0.0, ALU.mult,
                                             ALU.add).then_inc(s_gd, 1)
                dve.wait_ge(s_gd, 4)
                nc.vector.tensor_tensor(pre[0:N2, 1:8], sums[0:N2, 0:7], on4[0:N2, 1:8], ALU.mult).then_inc(s_gd, 1)
                dve.wait_ge(s_gd, 5)
                nc.vector.tensor_tensor(cumT[0:N2, :].rearrange("p (a b) -> p a b", b=16),
                                        inner[0:N2, :].rearrange("p (a b) -> p a b", b=16),
                                        pre[0:N2, :].unsqueeze(2).broadcast_to([N2, 8, 16]), ALU.add).then_inc(s_gd, 1)
                dve.wait_ge(s_gd, 6)
                nc.vector.tensor_tensor(gapT[0:N2, :].rearrange("p (a b) -> p a b", b=CHUNK),
                                        cumT[0:N2, CHUNK - 1:P:CHUNK].unsqueeze(2).broadcast_to([N2, 2, CHUNK]),
                                        cumT[0:N2, :].rearrange("p (a b) -> p a b", b=CHUNK),
                                        ALU.subtract).then_inc(s_gd, 1)
                dve.wait_ge(s_gp, 2)
                nc.vector.tensor_copy(cum[:, :, :].rearrange("p t h -> p (t h)"), bk[4][:, 0, 0:N2]).then_inc(s_gd, 1)
                nc.vector.tensor_copy(w2[:, :, :].rearrange("p t h -> p (t h)"), bk[4][:, 1, 0:N2]).then_inc(s_gd, 1)
                dve.wait_ge(s_ga, 1)
                nc.vector.tensor_scalar(zb[:, :, :], zb[:, :, :], 1.0, None, ALU.add).then_inc(s_gd, 1)
                dve.wait_ge(s_gd, 10)
                nc.vector.reciprocal(beta[:, :, :], zb[:, :, :]).then_inc(s_gd, 1)
                dve.wait_ge(s_gd, 11)
                dve.wait_ge(s_ga, 5)
                nc.vector.tensor_scalar(nbeta[:, :, :], beta[:, :, :], -1.0, None, ALU.mult).then_inc(s_gd, 1)
                nc.vector.tensor_tensor(bd[:, :, :], beta[:, :, :], dec[:, :, :], ALU.mult).then_inc(s_gd, 1)

        ORDER = [("p", 0), ("s", 0), ("p", 1), ("s", 1), ("p", 2), ("s", 2), ("p", 3), ("s", 3), ("d", 0), ("s", 4),
                 ("d", 1), ("s", 5), ("d", 2), ("d", 3), ("d", 4), ("d", 5), ("p", 4)]

        def run(eng, prepare, double, scan):

            def step(now, ahead):
                for kind, n in ORDER:
                    if kind == "p" and ahead:
                        prepare(*ahead, n)
                    if kind == "d" and ahead:
                        double(*ahead, n)
                    if kind == "s" and now:
                        scan(*now, n)

            step(None, (0, 0))
            with eng.Fori(0, NT // 2 - 1) as g:
                step((g, 0), (g, 1))
                step((g, 1), (g + 1, 0))
            step((NT // 2 - 1, 0), (NT // 2 - 1, 1))
            step((NT // 2 - 1, 1), None)

        with nc.Block() as block:

            @block.gpsimd
            def _(pool):
                def prepare(g, v, n):
                    t = 2 * g + v
                    if n == 0:
                        pool.wait_ge(s_T, freed(t, 1))
                        normalise(pool, nc.gpsimd, sc, xl[:, v:v + 1, :], Xv[:, bass.ds(g, 1), v, :], col1(rstd, g, v),
                                  col1(nmr, g, v), s_xh, made(t)).then_inc(s_xl, 1)
                        pool.wait_ge(s_xl, made(t))
                        sc.settle(pool)
                        nc.gpsimd.tensor_tensor(rk[:, :].rearrange("p (h d) -> p h d", h=2),
                                                xl[:, v, :].rearrange("p (h d) -> p h d", h=2), wide(col(rn, g, v)),
                                                ALU.mult).then_inc(s_rk, 1)
                        pool.wait_ge(s_crp, freed(t, 1))
                        sc.settle(pool)
                        nc.gpsimd.tensor_copy(cumt[:, :], col(cum, g, v)).then_inc(s_cumt, 1)
                        pool.wait_ge(s_x, freed(t, 2))
                        sc.settle(pool)
                        nc.gpsimd.tensor_tensor(xr[:, v, :], tile_of(Xv, g, v), xl[:, v, :], ALU.add).then_inc(s_xr, 1)
                    if n == 4:
                        pool.wait_ge(s_dr, made(t))
                        pool.wait_ge(s_rkx, made(t))
                        pool.wait_ge(s_o, freed(2 * t + 1, 4))
                        nc.gpsimd.tensor_tensor(rkd[:, v, :, :], rkx[:, :, 1:1 + P], drow[:, v, :, :],
                                                ALU.mult).then_inc(s_rkd, 1)

                run(pool, prepare, lambda g, v, n: None, lambda g, v, n: None)

            @block.tensor
            def _(pe):
                def prepare(g, v, n):
                    t = 2 * g + v
                    if n == 0:
                        pe.wait_ge(s_rk, made(t))
                        pe.wait_ge(s_rkx, freed(t, 1))
                        pe.wait_ge(s_xT, freed(t, 1))
                        for c in range(2):
                            nc.tensor.transpose(bk[0][:, c, :], xl[:, v, c * P:(c + 1) * P], ident[:, :])
                        for c in range(2):
                            i = nc.tensor.transpose(bk[0][:, 2 + c, :], rk[:, c * P:(c + 1) * P], ident[:, :])
                        i.then_inc(s_T, 1)
                    if n == 1:
                        pe.wait_ge(s_cumt, made(t))
                        pe.wait_ge(s_cr, freed(t, 1))
                        for h in range(2):
                            i = nc.tensor.matmul(bk[3][:, h, :], cumt[:, h:h + 1].broadcast_to([P, P]), ident[:, :],
                                                 start=True, stop=True)
                        i.then_inc(s_crp, 1)
                        pe.wait_ge(s_xT, made(t))
                        pe.wait_ge(s_rkx, made(t))
                        pe.wait_ge(s_wkt, freed(t, 1))
                        for c in range(2):
                            nc.tensor.matmul(bk[1][:, 0:2, :].rearrange("p a b -> p (a b)"), xT[:, c * P:(c + 1) * P],
                                             Ww[:, c, :], start=(c == 0), stop=(c == 1))
                        for h in range(2):
                            i = nc.tensor.transpose(bk[1][:, 2 + h, :], rkx[:, h, 0:P], ident[:, :])
                        i.then_inc(s_vw, 1)
                        pe.wait_ge(s_in, freed(t, 1))
                        for h in range(2):
                            nc.tensor.matmul(bk[2][:, h, :], rkx[:, h, 0:P], rkx[:, h, 0:P], start=True, stop=True)
                            i = nc.tensor.matmul(bk[2][:, 2 + h, :], rkx[:, h, 1:1 + P], rkx[:, h, 0:P], start=True,
                                                 stop=True)
                        i.then_inc(s_gr, 1)
                    if n == 3:
                        pe.wait_ge(s_M, made(t))
                        pe.wait_ge(s_in, made(t))
                        pe.wait_ge(s_PP, LEVELS * t + CREDIT)
                        for j in range(4):
                            i = nc.tensor.transpose(bk[4][:, j, :], Mi[:, j, :], ident[:, :])
                        i.then_inc(s_MI, 1)
                    if n == 4:
                        pe.wait_ge(s_AT, LEVELS * t + LEVELS + CREDIT)
                        pe.wait_ge(s_vs, made(t))
                        pe.wait_ge(s_wkd, made(t))
                        for h in range(2):
                            nc.tensor.matmul(bk[5][:, h, :], AT[:, LEVELS % 2, h, :], vsc[:, h, :], start=True, stop=True)
                            i = nc.tensor.matmul(bk[5][:, 2 + h, :], wkd[:, h, :], AT[:, LEVELS % 2, h, :], start=True,
                                                 stop=True)
                        i.then_inc(s_uwp, 1)

                def double(g, v, n):
                    t = 2 * g + v
                    if n < LEVELS:
                        k = LEVELS * t + n
                        if n == 0:
                            pe.wait_ge(s_MT, made(t))
                            pe.wait_ge(s_iT, made(t))
                            m = [Mi[:, h, :] for h in range(2)]
                            mT = [PP[:, 1, h, 1, :] for h in range(2)]
                        else:
                            pe.wait_ge(s_PP, k + CREDIT)
                            m = [PP[:, (n - 1) % 2, h, 0, :] for h in range(2)]
                            mT = [PP[:, (n - 1) % 2, h, 1, :] for h in range(2)]
                        for h in range(2):
                            nc.tensor.matmul(bk[4][:, 2 * h, :], mT[h], m[h], start=True, stop=True)
                            i = nc.tensor.matmul(bk[4][:, 2 * h + 1, :], m[h], mT[h], start=True, stop=True)
                        i.then_inc(s_sqp, 1)
                    if n >= 1:
                        k = LEVELS * t + n - 1
                        pe.wait_ge(s_PP, k + 1 + CREDIT)
                        if n == 1:
                            pe.wait_ge(s_A0, made(t))
                            pe.wait_ge(s_UW, freed(t, 1))
                        else:
                            pe.wait_ge(s_AT, k + CREDIT)
                        for h in range(2):
                            i = nc.tensor.matmul(bk[5][:, h, :], PP[:, (n - 1) % 2, h, 0, :], AT[:, (n - 1) % 2, h, :],
                                                 start=True, stop=True)
                        i.then_inc(s_atp, 1)

                def scan(g, v, n):
                    t = 2 * g + v
                    if n in (0, 2):
                        c = n // 2
                        rws = slice(CHUNK * c, CHUNK * (c + 1))
                        pe.wait_ge(s_UW, made(t))
                        if c == 0:
                            pe.wait_ge(s_S0, made(t))
                        else:
                            pe.wait_ge(s_S, made(2 * t))
                        for h in range(2):
                            i = nc.tensor.matmul(bk[6][rws, h, :], UW[:, v, (2 + h) * P + CHUNK * c:(2 + h) * P + CHUNK * (c + 1)],
                                                 S[:, h, :], start=True, stop=True)
                        i.then_inc(s_ws, 1)
                    if n in (1, 3):
                        c = n // 2
                        rws = slice(CHUNK * c, CHUNK * (c + 1))
                        pe.wait_ge(s_vn, made(2 * t + c))
                        pe.wait_ge(s_iT, made(t))
                        pe.wait_ge(s_wkt, made(t))
                        for h in range(2):
                            i = nc.tensor.matmul(bk[6][:, 2 + h, :], wkt[rws, v, h, :], vn[rws, h, :], start=True, stop=True)
                        i.then_inc(s_ds, 1)
                        pe.wait_ge(s_rkd, made(t))
                        if c == 0:
                            pe.wait_ge(s_x, freed(t, 1))
                        for h in range(2):
                            o = bk[7][:, h, CHUNK * c:CHUNK * (c + 1)]
                            nc.tensor.matmul(o, S[:, h, :], rkd[:, v, h, CHUNK * c:CHUNK * (c + 1)], start=True, stop=False)
                            i = nc.tensor.matmul(o, vn[rws, h, :], iT[rws, v, h, CHUNK * c:CHUNK * (c + 1)], start=False,
                                                 stop=True)
                        i.then_inc(s_o, 1)
                    if n == 5:
                        pe.wait_ge(s_oT, made(t))
                        for h in range(2):
                            i = nc.tensor.matmul(bk[7][:, 0:2, :].rearrange("p a b -> p (a b)"), oT[:, h, :], Wr[:, h, :],
                                                 start=(h == 0), stop=(h == 1))
                        i.then_inc(s_y, 1)

                run(pe, prepare, double, scan)

            @block.scalar
            def _(act):
                def prepare(g, v, n):
                    t = 2 * g + v
                    if n == 0:
                        act.wait_ge(s_gr, freed(t, 1))
                        act.wait_ge(s_rkd, freed(t, 1))
                        act.wait_ge(s_rkx, freed(t, 1))
                        nc.scalar.activation(rkx[:, :, 0:1], rkx[:, :, P:P + 1], ACT.Copy,
                                             scale=col1(flag, g, v)).then_inc(s_c0, 1)
                        act.wait_ge(s_T, made(t))
                        nc.scalar.activation(xT[:, :], bk[0][:, 0:2, :].rearrange("p a b -> p (a b)"),
                                             ACT.Copy).then_inc(s_xT, 1)
                        act.wait_ge(s_c0, made(t))
                        nc.scalar.activation(rkx[:, :, 1:1 + P], bk[0][:, 2:4, :], ACT.Copy).then_inc(s_rkx, 1)
                    if n == 1:
                        act.wait_ge(s_crp, made(t))
                        act.wait_ge(s_tmp, freed(t, 1))
                        act.wait_ge(s_dr, freed(t, 1))
                        nc.scalar.activation(cr[:, :, :], bk[3][:, 0:2, :], ACT.Copy).then_inc(s_cr, 1)
                        act.wait_ge(s_cr, made(t))
                        act.wait_ge(s_S, freed(2 * t + 1, 4))
                        act.wait_ge(s_rkd, freed(t, 2))
                        nc.scalar.activation(drow[:, v, :, :], cr[:, :, :], ACT.Exp).then_inc(s_dr, 1)
                    if n == 2:
                        act.wait_ge(s_tmp, made(t))
                        act.wait_ge(s_in, freed(t, 1))
                        nc.scalar.activation(L[:, :, :], tmp[:, :, :], ACT.Exp, scale=-1.0).then_inc(s_L, 1)
                    if n == 3:
                        act.wait_ge(s_MI, made(t))
                        act.wait_ge(s_atp, LEVELS * t + CREDIT)
                        nc.scalar.activation(PP[:, 1, :, 1, :], bk[4][:, 0:2, :], ACT.Copy).then_inc(s_MT, 1)
                        act.wait_ge(s_o, freed(2 * t + 1, 4))
                        nc.scalar.activation(iT[:, v, :, :], bk[4][:, 2:4, :], ACT.Copy).then_inc(s_iT, 1)
                    if n == 4:
                        act.wait_ge(s_uwp, made(t))
                        act.wait_ge(s_vn, freed(2 * t + 1, 4))
                        nc.scalar.activation(UW[:, v, :], bk[5][:, :, :].rearrange("p a b -> p (a b)"),
                                             ACT.Copy).then_inc(s_UW, 1)

                def double(g, v, n):
                    t = 2 * g + v
                    if n < LEVELS:
                        k = LEVELS * t + n
                        act.wait_ge(s_sqp, k + 1 + CREDIT)
                        if n == 1:
                            act.wait_ge(s_A0, made(t))
                        if n >= 2:
                            act.wait_ge(s_atp, k - 1 + CREDIT)
                        nc.scalar.activation(PP[:, n % 2, :, :, :].rearrange("p h s n -> p (h s n)"),
                                             bk[4][:, :, :].rearrange("p a b -> p (a b)"), ACT.Copy).then_inc(s_PP, 1)

                def scan(g, v, n):
                    t = 2 * g + v
                    if n == 4:
                        act.wait_ge(s_o, made(2 * t + 1))
                        act.wait_ge(s_y, freed(t, 1))
                        nc.scalar.activation(oT[:, :, :], bk[7][:, 0:2, :], ACT.Copy).then_inc(s_oT, 1)

                run(act, prepare, double, scan)

            @block.vector
            def _(dve):
                def prepare(g, v, n):
                    t = 2 * g + v
                    if n == 1:
                        dve.wait_ge(s_vw, made(t))
                        dve.wait_ge(s_uwp, freed(t, 1))
                        nc.vector.tensor_tensor(vsc[:, :, :], bk[1][:, 0:2, :], wide(col(beta, g, v)),
                                                ALU.mult).then_inc(s_vs, 1)
                        nc.vector.tensor_tensor(wkd[:, :, :], bk[1][:, 2:4, :], wide(col(bd, g, v)),
                                                ALU.mult).then_inc(s_wkd, 1)
                        dve.wait_ge(s_ds, freed(2 * t + 1, 4))
                        nc.vector.tensor_tensor(wkt[:, v, :, :], bk[1][:, 2:4, :], wide(col(tail, g, v)),
                                                ALU.mult).then_inc(s_wkt, 1)
                        dve.wait_ge(s_cr, made(t))
                        dve.wait_ge(s_L, freed(t, 1))
                        for h in range(2):
                            i = nc.vector.scalar_tensor_tensor(out=tmp[:, h, :], in0=cr[:, h, :], scalar=col(cum, g, v, h),
                                                               in1=msk[:, :], op0=ALU.subtract, op1=ALU.add)
                        i.then_inc(s_tmp, 1)
                    if n == 2:
                        dve.wait_ge(s_L, made(t))
                        dve.wait_ge(s_gr, made(t))
                        dve.wait_ge(s_sqp, LEVELS * t + CREDIT)
                        for h in range(2):
                            i = nc.vector.scalar_tensor_tensor(out=Mi[:, h, :], in0=bk[2][:, h, :],
                                                               scalar=col(nbeta, g, v, h), in1=L[:, h, :],
                                                               op0=ALU.mult, op1=ALU.mult)
                        i.then_inc(s_M, 1)
                        nc.vector.tensor_tensor(Mi[:, 2:4, :], bk[2][:, 2:4, :], L[:, :, :], ALU.mult).then_inc(s_in, 1)
                    if n == 3:
                        dve.wait_ge(s_MT, made(t))
                        dve.wait_ge(s_uwp, freed(t, 1))
                        nc.vector.tensor_tensor(AT[:, 0, :, :], PP[:, 1, :, 1, :],
                                                ident[:, :].unsqueeze(1).broadcast_to([P, 2, P]), ALU.add)\
                            .then_inc(s_A0, 1)

                def double(g, v, n):
                    t = 2 * g + v
                    if n >= 1:
                        k = LEVELS * t + n - 1
                        dve.wait_ge(s_atp, k + 1 + CREDIT)
                        dve.wait_ge(s_A0, made(t))
                        dve.wait_ge(s_AT, k + CREDIT)
                        nc.vector.tensor_tensor(AT[:, n % 2, :, :], AT[:, (n - 1) % 2, :, :], bk[5][:, 0:2, :],
                                                ALU.add).then_inc(s_AT, 1)

                def scan(g, v, n):
                    t = 2 * g + v
                    if n in (0, 2):
                        c = n // 2
                        rws = slice(CHUNK * c, CHUNK * (c + 1))
                        if c == 0:
                            dve.wait_ge(s_o, freed(2 * t + 1, 2))
                            dve.wait_ge(s_S, freed(2 * t + 1, 2))
                            nc.vector.tensor_scalar(S[:, :, :], S[:, :, :], col1(flag, g, v), None,
                                                    ALU.mult).then_inc(s_S0, 1)
                        dve.wait_ge(s_ws, made(2 * t + c))
                        dve.wait_ge(s_o, freed(2 * t + c, 2))
                        nc.vector.tensor_tensor(vn[rws, :, :], UW[rws, v, 0:2 * P].rearrange("p (h n) -> p h n", h=2),
                                                bk[6][rws, 0:2, :], ALU.subtract).then_inc(s_vn, 1)
                    if n in (1, 3):
                        c = n // 2
                        dve.wait_ge(s_ds, made(2 * t + c))
                        dve.wait_ge(s_o, made(2 * t + c))
                        dve.wait_ge(s_S0, made(t))
                        for h in range(2):
                            last = CHUNK * (c + 1) - 1
                            i = nc.vector.scalar_tensor_tensor(out=S[:, h, :], in0=S[:, h, :],
                                                               scalar=drow[:, v, h, last:last + 1], in1=bk[6][:, 2 + h, :],
                                                               op0=ALU.mult, op1=ALU.add)
                        i.then_inc(s_S, 1)
                    if n == 5:
                        dve.wait_ge(s_y, made(t))
                        dve.wait_ge(s_xr, made(t))
                        nc.vector.tensor_tensor(tile_of(Xv, g, v), xr[:, v, :],
                                                bk[7][:, 0:2, :].rearrange("p a b -> p (a b)"), ALU.add).then_inc(s_x, 1)

                run(dve, prepare, double, scan)


RH, RD = 16, 16
SOLVE_STEPS = 143
STRIPS = 4
STRIP_WIDTH = [RD - 4 * s + 1 for s in range(STRIPS)]
STRIP_START = [4 * sum(STRIP_WIDTH[:s]) for s in range(STRIPS)]
KK = 4 * sum(STRIP_WIDTH)
KKV = KK + RD * RD


def ridge_constants(B, T):
    i = np.arange(P)
    causal = np.where(i[None, :] >= i[:, None], 0.0, -1e30).astype(np.float32)
    carry = np.full((P, B * T // P), -1e30, np.float32)
    carry[P - 1, np.arange(B * T // P) % (T // P) != 0] = 0.0
    return {"causal": causal, "upto": (i[None, :] >= i[:, None]).astype(np.float32), "carry": carry}


def ridge_memory(nc, X, B, T, name, w, ident, identb, eps):
    NT = B * T // P
    with Scope(nc, name + "n") as stats, Scope(nc, name) as sc:
        rstd = stats.sb("rstd", [P, NT])
        nmr = stats.sb("nmr", [P, NT])
        with Scope(nc, name + "t") as temporary:
            norm_stats(nc, X, NT, rstd, nmr, temporary, eps)
        W = sc.sb("W", [P, 2, 4 * D])
        Wo = sc.sb("Wo", [P, 2, D])
        Wfb = sc.sb("Wfb", [P, 2, 2 * RH])
        nw = sc.sb("nw", [P, 2])
        mask = sc.sb("mask", [P, 4 * P], BF16)
        upto = sc.sb("upto", [P, P])
        carry = sc.sb("carry", [P, NT])
        delta = sc.sb("delta", [P, RH])
        lam = sc.sb("lam", [P, D])
        one = sc.sb("one", [P, 1])
        xl = sc.sb("xl", [P, D])
        xT = sc.sb("xT", [P, D])
        qk = sc.sb("qk", [P, 2, 2 * D])
        bk = sc.sb("bk", [P, 2, D])
        vv = sc.sb("vv", [P, 2, D])
        ga = sc.sb("ga", [P, 2, D])
        gb = sc.sb("gb", [P, 2, D])
        ss = sc.sb("ss", [P, 2 * RH])
        rn = sc.sb("rn", [P, 2 * RH])
        zf, zw, lf, be, gs, gr = [sc.sb(n, [P, RH]) for n in ("zf", "zw", "lf", "be", "gs", "gr")]
        cum = sc.sb("cum", [P, 2, RH])
        ncum = sc.sb("ncum", [P, 2, RH])
        E = sc.sb("E", [P, 2, 4, P])
        Dk = sc.sb("D", [P, 2, 4, P])
        R = sc.sb("R", [P, 2, 2, KKV])
        Hs = sc.sb("H", [P, 2, RH, KKV])
        A = sc.sb("A", [P, RH, KK])
        pr = sc.sb("pr", [P, RH, 156])
        L = sc.sb("L", [P, RH, RD - 1, RD - 1])
        piv = sc.sb("piv", [P, RH, RD])
        x = sc.sb("x", [P, RH, RD])
        Po = sc.sb("Po", [P, 4, RD, RD])
        o = sc.sb("o", [P, D])
        og = sc.sb("og", [P, D])
        og2 = sc.sb("og2", [P, D])
        oT = sc.sb("oT", [P, D])
        bT, bqk, bvg, bfb, brow, bH0, bH1, bY = [sc.ps(f"b{i}", [P, 4 * P]) for i in range(8)]
        bH = (bH0, bH1)
        (s_xl, s_T, s_xT, s_pj, s_zf, s_sq, s_ss, s_rn, s_l1, s_lf, s_cp, s_cum, s_be, s_qk, s_v, s_g, s_gb, s_rw,
         s_E, s_mk, s_D, s_R, s_Hp, s_H, s_y, s_el, s_x, s_op, s_o, s_og, s_rr, s_og2, s_oT, s_oTc, s_yo, s_X) = [
             sc.sem(n) for n in (
                 "xl", "T", "xT", "pj", "zf", "sq", "ss", "rn", "l1", "lf", "cp", "cum", "be", "qk", "v", "g", "gb",
                 "rw", "E", "mk", "D", "R", "Hp", "H", "y", "el", "x", "op", "o", "og", "rr", "og2", "oT", "oTc",
                 "yo", "X")]
        with Scope(nc, name + "w") as ws:
            w1T, w2, maskf = xl[0:RD, :], oT[0:RD, :], og2[:, 0:P]
            s_w = ws.sem("w")
            s_wp = ws.sem("wp")
            s_wa = ws.sem("wa")
            ws.arm([(W[:, :, 0:D], rows(w["wq"])), (W[:, :, D:2 * D], rows(w["wk"])), (W[:, :, 2 * D:3 * D], rows(w["wv"])),
                    (Wo[:, :, :], rows(w["wo"])), (Wfb[:, :, :], rows(w["wfb"])), (nw[:, :], w["nw"]),
                    (upto[:, :], w["upto"]), (carry[:, :], w["carry"][:, 0:NT]), (delta[:, :], spread(w["delta"])),
                    (lam[:, :], spread(w["lam"])), (w1T, w["w1T"]), (w2, w["w2"]),
                    (maskf, w["causal"])])
            sc.arm([])
            with nc.Block() as block:

                @block.vector
                def _(dve):
                    for j in range(4):
                        nc.vector.tensor_copy(mask[:, j * P:(j + 1) * P], maskf)
                    for c in range(2):
                        nc.vector.tensor_scalar(Wo[:, c, :], Wo[:, c, :], nw[:, c:c + 1], None, ALU.mult)
                    nc.vector.memset(one[:, :], 1.0).then_inc(s_w, 1)
                    nc.vector.memset(Hs[:, :, :, :], 0.0)
                    nc.vector.memset(R[:, :, :, :], 0.0).then_inc(s_w, 1)
                    nc.vector.scalar_tensor_tensor(out=og[:, :], in0=lam[:, :], scalar=-1.0, in1=lam[:, :],
                                                   op0=ALU.mult, op1=ALU.min).then_inc(s_w, 1)
                    dve.wait_ge(s_wa, CREDIT + 2)
                    nc.vector.scalar_tensor_tensor(out=lam[:, :], in0=lam[:, :], scalar=0.0, in1=og[:, :],
                                                   op0=ALU.max, op1=ALU.add).then_inc(s_w, 1)
                    dve.wait_ge(s_w, CREDIT + 4)
                    nc.vector.tensor_scalar(lam[:, :], lam[:, :], 0.25, None, ALU.add).then_inc(s_w, 1)

                @block.tensor
                def _(pe):
                    for c in range(2):
                        i = nc.tensor.matmul(bT[:, c * D:(c + 1) * D], w1T[:, c * P:(c + 1) * P], w2, start=True,
                                             stop=True)
                    i.then_inc(s_wp, 1)

                @block.scalar
                def _(act):
                    act.wait_ge(s_w, CREDIT + 3)
                    nc.scalar.activation(og[:, :], og[:, :], ACT.Exp).then_inc(s_wa, 1)
                    act.wait_ge(s_wa, CREDIT + 1)
                    nc.scalar.activation(og[:, :], og[:, :], ACT.Ln, bias=one[:, 0:1]).then_inc(s_wa, 1)
                    act.wait_ge(s_wp, CREDIT + 1)
                    nc.scalar.activation(W[:, :, 3 * D:4 * D], bT[:, :].rearrange("p (c n) -> p c n", c=2),
                                         ACT.Copy).then_inc(s_wa, 1)


        def tile(t):
            return flat(X[:, bass.ds(t, 1), :])

        def strip(a, s):
            w_ = STRIP_WIDTH[s]
            return a[:, :, STRIP_START[s]:STRIP_START[s] + 4 * w_].rearrange("p h (r c) -> p h r c", r=4)

        def heads(a):
            return a.rearrange("p (h d) -> p h d", d=RD)

        def walk(eng, stages):

            def step(t, p, at_=None):
                n = t if at_ is None else at_
                stages(t, p, {"front": n + 2 < NT, "memory": 0 <= n + 1 < NT, "solve": 0 <= n < NT,
                              "out": 0 <= n - 1, "add": 0 <= n - 2})

            for t in (-2, -1, 0, 1):
                step(t, t % 2)
            with eng.Fori(0, (NT - 4) // 2) as g:
                step(2 * g + 2, 0, 2)
                step(2 * g + 3, 1, 2)
            for t in (NT - 2, NT - 1, NT):
                step(t, t % 2)

        with nc.Block() as block:

            @block.gpsimd
            def _(pool):
                def outputs(t, p):
                    k = Count(20 * t + CREDIT)
                    pool.wait_ge(s_x, made(t))
                    pool.wait_ge(s_og, 3 * t + CREDIT)
                    for u in range(4):
                        hh = slice(4 * u, 4 * u + 4)
                        pool.wait_ge(s_op, k.made())
                        kv = Hs[:, p, hh, KK:KKV].rearrange("p h (i j) -> p h i j", i=RD)
                        nc.gpsimd.tensor_tensor(Po[:, :, :, :], kv, x[:, hh, :].unsqueeze(3).broadcast_to([P, 4, RD, RD]),
                                                ALU.mult).then_inc(s_op, k.one())
                        for m in (8, 4, 2):
                            pool.wait_ge(s_op, k.made())
                            nc.gpsimd.tensor_tensor(Po[:, :, 0:m, :], Po[:, :, 0:m, :], Po[:, :, m:2 * m, :],
                                                    ALU.add).then_inc(s_op, k.one())
                        pool.wait_ge(s_op, k.made())
                        i = nc.gpsimd.tensor_tensor(heads(o[:, :])[:, hh, :], Po[:, :, 0, :], Po[:, :, 1, :],
                                                    ALU.add)
                        i.then_inc(s_op, k.one())
                    pool.wait_ge(s_op, k.made())
                    nc.gpsimd.sem_inc(s_o, 1)

                def products(t, p, pairs):
                    pool.wait_ge(s_qk, 2 * t + 2 + CREDIT)
                    pool.wait_ge(s_v, made(t))
                    q_, k_, b_, v_ = heads(qk[:, p, 0:D]), heads(qk[:, p, D:2 * D]), heads(bk[:, p, :]), heads(vv[:, p, :])
                    for r in pairs:
                        hh = slice(2 * r, 2 * r + 2)
                        pool.wait_ge(s_Hp, 16 * t + 2 * r - 2 + CREDIT)
                        Rr = R[:, r % 2, :, :]
                        for s in range(STRIPS):
                            wd = STRIP_WIDTH[s] - 1
                            nc.gpsimd.tensor_tensor(
                                strip(Rr, s)[:, :, :, 0:wd],
                                b_[:, hh, 4 * s:4 * s + 4].unsqueeze(3).broadcast_to([P, 2, 4, wd]),
                                k_[:, hh, 4 * s:RD].unsqueeze(2).broadcast_to([P, 2, 4, wd]), ALU.mult)
                        nc.gpsimd.tensor_tensor(
                            Rr[:, :, KK:KKV].rearrange("p h (i j) -> p h i j", i=RD),
                            b_[:, hh, :].unsqueeze(3).broadcast_to([P, 2, RD, RD]),
                            v_[:, hh, :].unsqueeze(2).broadcast_to([P, 2, RD, RD]), ALU.mult).then_inc(s_R, 1)

                def stages(t, p, do):
                    if do["memory"]:
                        products(t + 1, 1 - p, range(2))
                    if do["out"]:
                        outputs(t - 1, 1 - p)
                    if do["memory"]:
                        products(t + 1, 1 - p, range(2, RH // 2))

                walk(pool, stages)

            @block.tensor
            def _(pe):
                def transposes(t):
                    pe.wait_ge(s_xl, made(t))
                    pe.wait_ge(s_oTc, made(t - 4))
                    for c in range(2):
                        i = nc.tensor.transpose(bT[:, c * P:(c + 1) * P], xl[:, c * P:(c + 1) * P], ident[:, :])
                    i.then_inc(s_T, 1)

                def projections(t):
                    pe.wait_ge(s_xT, made(t))
                    pe.wait_ge(s_qk, 2 * t + CREDIT)
                    pe.wait_ge(s_g, 3 * t + CREDIT)
                    pe.wait_ge(s_v, made(t - 1))
                    pe.wait_ge(s_cum, 2 * t + CREDIT)
                    for out, wt in ((bqk[:, :], W[:, :, 0:2 * D]), (bvg[:, :], W[:, :, 2 * D:4 * D]),
                                    (bfb[:, 0:2 * RH], Wfb[:, :, :])):
                        for c in range(2):
                            i = nc.tensor.matmul(out, xT[:, c * P:(c + 1) * P], wt[:, c, :], start=(c == 0), stop=(c == 1))
                    i.then_inc(s_pj, 1)

                def cumulate(t):
                    pe.wait_ge(s_lf, made(t))
                    nc.tensor.matmul(bfb[:, 64:64 + RH], upto[:, :], lf[:, :], start=True, stop=True).then_inc(s_cp, 1)

                def rows_of(p, u, masked):
                    if masked:
                        nc.tensor.matmul(brow[:, :], identb[:, :], mask[:, :], start=True, stop=False)
                    for j in range(4):
                        i = nc.tensor.matmul(brow[:, j * P:(j + 1) * P],
                                             cum[:, p, 4 * u + j:4 * u + j + 1].broadcast_to([P, P]), ident[:, :],
                                             start=(j == 0 and not masked), stop=(j == 3))
                    return i

                def row_sums(t, p, u):
                    pe.wait_ge(s_cum, 2 * t + 2 + CREDIT)
                    pe.wait_ge(s_D, 4 * t + u + CREDIT)
                    rows_of(p, u, False).then_inc(s_rw, 1)

                def hide(t, p, u):
                    pe.wait_ge(s_E, 4 * t + u + 1 + CREDIT)
                    rows_of(p, u, True).then_inc(s_mk, 1)

                def memories(t, p, u):
                    pe.wait_ge(s_D, 4 * t + u + 1 + CREDIT)
                    if u == 0:
                        pe.wait_ge(s_y, 4 * t + CREDIT)
                    for j in range(4):
                        h = 4 * u + j
                        pe.wait_ge(s_R, 8 * t + h // 2 + 1 + CREDIT)
                        pe.wait_ge(s_H, 16 * t + h - 1 + CREDIT)
                        nc.tensor.matmul(bH[h % 2][:, 0:KKV], Dk[:, u % 2, j, :], R[:, (h // 2) % 2, h % 2, :], start=True,
                                         stop=False)
                        nc.tensor.matmul(bH[h % 2][:, 0:KKV], E[:, u % 2, j, :], Hs[:, 1 - p, h, :], start=False,
                                         stop=True).then_inc(s_Hp, 1)

                def project_out(t, fronts):
                    pe.wait_ge(s_og2, made(t))
                    pe.wait_ge(s_xT, made(fronts))
                    for c in range(2):
                        i = nc.tensor.transpose(bT[:, c * P:(c + 1) * P], og2[:, c * P:(c + 1) * P], ident[:, :])
                    i.then_inc(s_oT, 1)
                    pe.wait_ge(s_oTc, made(t))
                    pe.wait_ge(s_X, made(t - 1))
                    for c in range(2):
                        i = nc.tensor.matmul(bY[:, 0:D], oT[:, c * P:(c + 1) * P], Wo[:, c, :], start=(c == 0), stop=(c == 1))
                    i.then_inc(s_yo, 1)

                def stages(t, p, do):
                    if do["front"]:
                        transposes(t + 2)
                        projections(t + 2)
                    if do["memory"]:
                        row_sums(t + 1, 1 - p, 0)
                        hide(t + 1, 1 - p, 0)
                        for u in range(4):
                            if u < 3:
                                row_sums(t + 1, 1 - p, u + 1)
                                hide(t + 1, 1 - p, u + 1)
                            memories(t + 1, 1 - p, u)
                            if u == 1 and do["front"]:
                                cumulate(t + 2)
                    elif do["front"]:
                        cumulate(t + 2)
                    if do["out"]:
                        project_out(t - 1, t + 2 if do["front"] else NT - 1)

                walk(pe, stages)

            @block.scalar
            def _(act):
                def exp(out, in_, sem, **kw):
                    nc.scalar.activation(out, in_, ACT.Exp, **kw).then_inc(sem, 1)

                def inputs(t, p):
                    act.wait_ge(s_T, made(t - 1))
                    nc.scalar.activation(xl[:, :], tile(t), ACT.Identity, scale=rstd[:, bass.ds(t, 1)],
                                         bias=nmr[:, bass.ds(t, 1)]).then_inc(s_xl, 1)
                    act.wait_ge(s_T, made(t))
                    act.wait_ge(s_pj, made(t - 1))
                    nc.scalar.activation(xT[:, :], bT[:, 0:D], ACT.Copy).then_inc(s_xT, 1)

                def gates(t, p):
                    act.wait_ge(s_pj, made(t))
                    if not isinstance(t, int) or t > 0:
                        act.wait_ge(s_R, 8 * t - 8 + CREDIT)
                    nc.scalar.activation(qk[:, p, :], bqk[:, :], ACT.Square).then_inc(s_sq, 1)
                    nc.scalar.activation(vv[:, p, :], bvg[:, 0:D], ACT.Copy).then_inc(s_v, 1)
                    exp(ga[:, p, :], bvg[:, D:2 * D], s_g, scale=-1.0)
                    act.wait_ge(s_zf, 3 * t + 3 + CREDIT)
                    exp(be[:, :], be[:, :], s_be, scale=-1.0)
                    exp(zw[:, :], zw[:, :], s_l1)
                    act.wait_ge(s_be, 3 * t + 1 + CREDIT)
                    nc.scalar.activation(be[:, :], be[:, :], ACT.Ln, bias=one[:, 0:1]).then_inc(s_be, 1)
                    act.wait_ge(s_g, 3 * t + 1 + CREDIT)
                    nc.scalar.activation(ga[:, p, :], ga[:, p, :], ACT.Ln, bias=one[:, 0:1]).then_inc(s_g, 1)
                    act.wait_ge(s_l1, 2 * t + 1 + CREDIT)
                    nc.scalar.activation(zw[:, :], zw[:, :], ACT.Ln, bias=one[:, 0:1]).then_inc(s_l1, 1)
                    act.wait_ge(s_be, 3 * t + 2 + CREDIT)
                    exp(be[:, :], be[:, :], s_be, scale=-1.0)
                    act.wait_ge(s_g, 3 * t + 2 + CREDIT)
                    exp(ga[:, p, :], ga[:, p, :], s_g, scale=-1.0)
                    act.wait_ge(s_ss, made(t))
                    nc.scalar.activation(rn[:, :], ss[:, :], ACT.Ln, bias=eps[:, 1:2]).then_inc(s_rn, 1)
                    act.wait_ge(s_rn, 2 * t + 1 + CREDIT)
                    exp(rn[:, :], rn[:, :], s_rn, scale=-0.5)

                def decays(t, p, u):
                    act.wait_ge(s_rw, 4 * t + u + 1 + CREDIT)
                    act.wait_ge(s_Hp, 16 * t + 4 * u - 4 + CREDIT)
                    sc.settle(act)
                    exp(flat(E[:, u % 2, :, :]), brow[:, :], s_E, bias=carry[:, bass.ds(t, 1)])
                    act.wait_ge(s_mk, 4 * t + u + 1 + CREDIT)
                    for j in range(4):
                        h = 4 * u + j
                        i = nc.scalar.activation(Dk[:, u % 2, j, :], brow[:, j * P:(j + 1) * P], ACT.Exp,
                                                 bias=ncum[:, p, h:h + 1])
                    i.then_inc(s_D, 1)

                def keep(t, p, u):
                    if u == 0:
                        act.wait_ge(s_o, made(t - 2))
                    for j in range(4):
                        h = 4 * u + j
                        act.wait_ge(s_Hp, 16 * t + h + 1 + CREDIT)
                        nc.scalar.activation(Hs[:, p, h, :], bH[h % 2][:, 0:KKV], ACT.Copy).then_inc(s_H, 1)

                def rms(t):
                    act.wait_ge(s_og, 3 * t + 3 + CREDIT)
                    nc.scalar.activation(gr[:, :], gs[:, :], ACT.Ln, scale=1.0 / RD, bias=eps[:, 0:1]).then_inc(s_rr, 1)
                    act.wait_ge(s_rr, 2 * t + 1 + CREDIT)
                    exp(gr[:, :], gr[:, :], s_rr, scale=-0.5)

                def right_sides(t, p):
                    act.wait_ge(s_H, 16 * t + 16 + CREDIT)
                    act.wait_ge(s_qk, 2 * t + 2 + CREDIT)
                    for s in range(STRIPS):
                        nc.scalar.activation(strip(Hs[:, p, :, :], s)[:, :, :, STRIP_WIDTH[s] - 1],
                                             heads(qk[:, p, 0:D])[:, :, 4 * s:4 * s + 4], ACT.Copy).then_inc(s_y, 1)

                def stages(t, p, do):
                    if do["solve"]:
                        act.wait_ge(s_g, 3 * t + 3 + CREDIT)
                        act.wait_ge(s_og, 3 * t - 3 + CREDIT)
                        nc.scalar.activation(gb[:, p, :], ga[:, p, :], ACT.Copy).then_inc(s_gb, 1)
                    if do["front"]:
                        inputs(t + 2, p)
                    if do["memory"]:
                        decays(t + 1, 1 - p, 0)
                    if do["memory"]:
                        decays(t + 1, 1 - p, 1)
                        if do["front"]:
                            gates(t + 2, p)
                        for u in range(4):
                            keep(t + 1, 1 - p, u)
                            if u < 2:
                                decays(t + 1, 1 - p, u + 2)
                            if u == 2 and do["out"]:
                                rms(t - 1)
                        right_sides(t + 1, 1 - p)
                    elif do["front"]:
                        gates(t + 2, p)
                    if do["out"]:
                        if not do["memory"]:
                            rms(t - 1)
                        act.wait_ge(s_oT, made(t - 1))
                        act.wait_ge(s_yo, made(t - 2))
                        nc.scalar.activation(oT[:, :], bT[:, 0:D], ACT.Copy).then_inc(s_oTc, 1)

                walk(act, stages)

            @block.vector
            def _(dve):
                tt = nc.vector.tensor_tensor

                def gate_inputs(t, p):
                    dve.wait_ge(s_pj, made(t))
                    tt(zf[:, :], bfb[:, 0:RH], delta[:, :], ALU.add).then_inc(s_zf, 1)
                    nc.vector.tensor_copy(be[:, :], bfb[:, RH:2 * RH]).then_inc(s_zf, 1)
                    dve.wait_ge(s_zf, 3 * t + 2 + CREDIT)
                    nc.vector.scalar_tensor_tensor(out=zw[:, :], in0=zf[:, :], scalar=-1.0, in1=zf[:, :], op0=ALU.mult,
                                                   op1=ALU.min).then_inc(s_zf, 1)

                def squares(t, p):
                    dve.wait_ge(s_sq, made(t))
                    nc.vector.reduce_sum(ss[:, :], heads(qk[:, p, :]), axis=AX).then_inc(s_ss, 1)

                def log_decay(t, p):
                    dve.wait_ge(s_l1, 2 * t + 2 + CREDIT)
                    nc.vector.scalar_tensor_tensor(out=lf[:, :], in0=zf[:, :], scalar=0.0, in1=zw[:, :], op0=ALU.min,
                                                   op1=ALU.subtract).then_inc(s_lf, 1)

                def keys(t, p):
                    dve.wait_ge(s_rn, 2 * t + 2 + CREDIT)
                    dve.wait_ge(s_ss, made(t))
                    tt(heads(qk[:, p, :]), heads(bqk[:, :]), rn[:, :].unsqueeze(2).broadcast_to([P, 2 * RH, RD]),
                       ALU.mult).then_inc(s_qk, 1)
                    dve.wait_ge(s_qk, 2 * t + 1 + CREDIT)
                    dve.wait_ge(s_be, 3 * t + 3 + CREDIT)
                    tt(heads(bk[:, p, :]), heads(qk[:, p, D:2 * D]), be[:, :].unsqueeze(2).broadcast_to([P, RH, RD]),
                       ALU.mult).then_inc(s_qk, 1)

                def sums(t, p):
                    dve.wait_ge(s_cp, made(t))
                    dve.wait_ge(s_D, 4 * t - 4 + CREDIT)
                    nc.vector.tensor_copy(cum[:, p, :], bfb[:, 64:64 + RH]).then_inc(s_cum, 1)
                    nc.vector.tensor_scalar(ncum[:, p, :], bfb[:, 64:64 + RH], -1.0, None, ALU.mult).then_inc(s_cum, 1)

                def gated(t, p):
                    dve.wait_ge(s_o, made(t))
                    dve.wait_ge(s_gb, made(t))
                    tt(og[:, :], o[:, :], gb[:, p, :], ALU.mult).then_inc(s_og, 1)
                    dve.wait_ge(s_og, 3 * t + 1 + CREDIT)
                    dve.wait_ge(s_oT, made(t - 1))
                    tt(og2[:, :], og[:, :], og[:, :], ALU.mult).then_inc(s_og, 1)
                    dve.wait_ge(s_og, 3 * t + 2 + CREDIT)
                    nc.vector.reduce_sum(gs[:, :], heads(og2[:, :]), axis=AX).then_inc(s_og, 1)

                def normed(t, p):
                    dve.wait_ge(s_rr, 2 * t + 2 + CREDIT)
                    dve.wait_ge(s_og, 3 * t + 3 + CREDIT)
                    tt(heads(og2[:, :]), heads(og[:, :]), gr[:, :].unsqueeze(2).broadcast_to([P, RH, RD]),
                       ALU.mult).then_inc(s_og2, 1)

                def residual(t):
                    dve.wait_ge(s_yo, made(t))
                    tt(tile(t), tile(t), bY[:, 0:D], ALU.add).then_inc(s_X, 1)

                def solve(t, p, between):
                    n = Count(SOLVE_STEPS * t + CREDIT)
                    dve.wait_ge(s_y, 4 * t + 4 + CREDIT)
                    dve.wait_ge(s_el, n.made())
                    tt(piv[:, :, 0], Hs[:, p, :, 0], heads(lam[:, :])[:, :, 0], ALU.add).then_inc(s_el, n.one())
                    def row(k):
                        return strip(Hs[:, p, :, 0:KK] if k == 0 else A[:, :, :], k // 4)[:, :, k % 4, k % 4:]

                    def invert(k, after):
                        dve.wait_ge(s_el, after)
                        nc.vector.reciprocal(piv[:, :, k], piv[:, :, 0] if k == 0 else row(k)[:, :, 0])\
                            .then_inc(s_el, n.one())

                    def scale(k, after):
                        dve.wait_ge(s_el, after)
                        tt(L[:, :, k, k:], row(k)[:, :, 1:RD - k], piv[:, :, k:k + 1].broadcast_to([P, RH, RD - k - 1]),
                           ALU.mult).then_inc(s_el, n.one())

                    invert(0, n.made())
                    scale(0, n.made())
                    for k in range(RD - 1):
                        s0, r = k // 4, k % 4
                        src = Hs[:, p, :, 0:KK] if k == 0 else A[:, :, :]
                        dve.wait_ge(s_el, n.made())
                        start = 0
                        parts = []
                        for s in range(s0, STRIPS):
                            first = r + 1 if s == s0 else 0
                            if first == 4:
                                continue
                            c0 = 4 * s + first
                            nr, ncol = 4 - first, RD + 1 - c0
                            prod = pr[:, :, start:start + nr * ncol].rearrange("p h (r c) -> p h r c", r=nr)
                            start += nr * ncol
                            tt(prod, L[:, :, k, c0 - 1:c0 - 1 + nr].unsqueeze(3).broadcast_to([P, RH, nr, ncol]),
                               row(k)[:, :, c0 - k:].unsqueeze(2).broadcast_to([P, RH, nr, ncol]),
                               ALU.mult).then_inc(s_el, n.one())
                            parts.append((s, first, prod, n.made()))
                        for i, (s, first, prod, ready) in enumerate(parts):
                            dve.wait_ge(s_el, ready)
                            tt(strip(A, s)[:, :, first:, first:], strip(src, s)[:, :, first:, first:], prod,
                               ALU.subtract).then_inc(s_el, n.one())
                            if i == 0:
                                next_row = n.made()
                            if k > 0 and i == min(1, len(parts) - 1):
                                invert(k + 1, next_row)
                                inverted = n.made()
                            if 0 < k < RD - 2 and i == min(2, len(parts) - 1):
                                scale(k + 1, inverted)
                        if k == 0:
                            dve.wait_ge(s_el, n.made())
                            for s in range(STRIPS):
                                r0 = 1 if s == 0 else 0
                                w_ = STRIP_WIDTH[s]
                                diag = A[:, :, STRIP_START[s] + r0 * (w_ + 1):STRIP_START[s] + 4 * w_:w_ + 1]
                                tt(diag, diag, heads(lam[:, :])[:, :, 4 * s + r0:4 * s + 4], ALU.add).then_inc(s_el, n.one())
                            invert(1, n.made())
                            scale(1, n.made())
                        for work in between.get(k, []):
                            work()
                    dve.wait_ge(s_el, n.made())
                    dve.wait_ge(s_o, made(t - 1))
                    tt(x[:, :, 0], Hs[:, p, :, STRIP_WIDTH[0] - 1], piv[:, :, 0], ALU.mult).then_inc(s_el, n.one())
                    for s in range(STRIPS):
                        r0 = 1 if s == 0 else 0
                        tt(x[:, :, 4 * s + r0:4 * s + 4], strip(A, s)[:, :, r0:, STRIP_WIDTH[s] - 1],
                           piv[:, :, 4 * s + r0:4 * s + 4], ALU.mult).then_inc(s_el, n.one())
                    for k in range(RD - 1, 0, -1):
                        dve.wait_ge(s_el, n.made())
                        tt(pr[:, :, 0:k], L[:, :, 0:k, k - 1], x[:, :, k:k + 1].broadcast_to([P, RH, k]),
                           ALU.mult).then_inc(s_el, n.one())
                        dve.wait_ge(s_el, n.made())
                        i = tt(x[:, :, 0:k], x[:, :, 0:k], pr[:, :, 0:k], ALU.subtract)
                        i.then_inc(s_el, n.one())
                    dve.wait_ge(s_el, n.made())
                    dve.sem_inc(s_x, 1)
                    assert n.n == SOLVE_STEPS, n.n

                def stages(t, p, do):
                    between = {k: [] for k in (0, 1, 3, 6, 8, 12)}
                    if do["front"]:
                        u = t + 2
                        between[1] += [lambda: gate_inputs(u, p), lambda: squares(u, p)]
                        between[3] += [lambda: log_decay(u, p), lambda: keys(u, p)]
                        between[8] += [lambda: sums(u, p)]
                    if do["add"]:
                        between[1] += [lambda: residual(t - 2)]
                    if do["out"]:
                        between[6] += [lambda: gated(t - 1, 1 - p)]
                        between[12] += [lambda: normed(t - 1, 1 - p)]
                    if do["solve"]:
                        solve(t, p, between)
                    else:
                        for k in sorted(between):
                            for f in between[k]:
                                f()
                    if not do["solve"] and do["out"]:
                        residual(t - 1)

                walk(dve, stages)


def spaced_rows(wo, row):
    out = np.zeros((P, 4, D), wo.dtype)
    for g in range(4):
        for i in range(4):
            out[32 * i:32 * i + HD, g] = wo[row(g, i) * HD:(row(g, i) + 1) * HD]
    return out


def bfloat16_bits(constant):
    return (np.ascontiguousarray(constant).view(np.uint32) >> 16).astype(np.uint16)


def attention_constants(local):
    c = {}
    for name, parts in (("selq", Q_PARTS), ("selk", K_PARTS)):
        s = np.zeros((P, 3, 8, STACK), np.float32)
        for h in range(8):
            for block, a in enumerate(parts):
                for d in range(HD):
                    s[HD * h + d, a, h, HD * block + d] = 1
        c[name] = bfloat16_bits(s)
    sels = np.zeros((P, P), np.float32)
    for r in range(P):
        sels[32 * (r // 32) + HD, r] = 1
    minus = np.zeros((P, HEADS), np.float32)
    for h in range(HEADS):
        minus[96 + h, h] = minus[112 + h, h] = -1
    c.update(sels=sels, minus=bfloat16_bits(minus))
    if local:
        i, k = np.arange(P)[:, None], np.arange(2 * P)[None, :]
        m = np.zeros((3, P, 2 * P), np.float32)
        for v in range(3):
            ok = (k >= i) & (k <= i + 2 * KEYS_WINDOW)
            if v == 0:
                ok &= k >= KEYS_WINDOW
            if v == 2:
                ok &= k < 2 * P - KEYS_WINDOW
            m[v][~ok] = -1e30
        mt = m.reshape(3, P, 2, P).transpose(0, 3, 2, 1).reshape(3, P, 2 * P)
        c.update(mask=bfloat16_bits(m.transpose(1, 0, 2)),
                 maskT=bfloat16_bits(mt.transpose(1, 0, 2)))
    return c


def delta_constants():
    i, j = np.arange(P)[:, None], np.arange(P)[None, :]
    same = i // CHUNK == j // CHUNK
    flag = np.ones(64, np.float32)
    flag[::8] = 0
    return {"on32": (np.arange(D) % 32 != 0).astype(np.float32),
            "on16": (np.arange(P) % 16 != 0).astype(np.float32), "on4": (np.arange(8) % 4 != 0).astype(np.float32),
            "msk": np.where(same & (j < i), 0.0, 1e30).astype(np.float32), "flag": flag}


def lay_out(w):
    return {
        "tr_weightT": w["L1_ffn_weight"].T, "tr_aux1": w["L1_ffn_aux_weight1"], "tr_aux2": w["L1_ffn_aux_weight2"],
        "tr_bias": w["L1_ffn_bias"],
        **{"ff_" + n: w["L0_ffn_" + n] for n in ("Wq", "bq", "Wdown", "bdown", "Wup", "bup", "Wo", "bo",
                                                 "Wg", "bg", "We")},
        "ff_gammas": np.stack([w[n].reshape(2, P).T for n in ("L0_ffn_gamma1", "L0_ffn_gamma2")], axis=-1),
        "ga_wq": w["L1_attn_b_Wq"], "ga_wk": w["L1_attn_b_Wk"], "ga_wv": w["L1_attn_b_Wv"],
        "ga_wo": spaced_rows(w["L1_attn_b_Wo"], lambda g, i: 4 * i + g),
        "ga_bq": w["L1_attn_b_bq"].reshape(2, P).T, "ga_bk": w["L1_attn_b_bk"].reshape(1, 64).T,
        "ga_bv": w["L1_attn_b_bv"], "ga_bo": w["L1_attn_b_bo"],
        "sa_wq": w["L1_attn_a_wq"].T, "sa_wk": w["L1_attn_a_wk"].T, "sa_wv": w["L1_attn_a_wv"].T,
        "sa_wo": spaced_rows(w["L1_attn_a_wo"].T, lambda g, i: 4 * g + i),
        "sa_bq": w["L1_attn_a_bq"].reshape(2, P).T, "sa_bk": w["L1_attn_a_bk"].reshape(2, P).T,
        "sa_bv": w["L1_attn_a_bv"], "sa_bo": w["L1_attn_a_bo"],
        **{"ga_" + n: v for n, v in attention_constants(False).items()},
        **{"sa_" + n: v for n, v in attention_constants(True).items()},
        "dr_wwT": w["L0_attn_a_W_write"].T, "dr_wrT": w["L0_attn_a_W_read"].T,
        "dr_wab": np.concatenate([w["L0_attn_a_W_alpha"], w["L0_attn_a_W_beta"]]).T,
        "dr_walpha": w["L0_attn_a_W_alpha"], "dr_dtb": w["L0_attn_a_dt_bias"], "dr_alog": w["L0_attn_a_A_log"],
        **{"dr_" + n: v for n, v in delta_constants().items()},
        **{"rm_" + n: w["L0_attn_b_" + m] for n, m in (("wq", "Wq"), ("wk", "Wk"), ("wv", "Wv"), ("wo", "Wo"),
                                                      ("delta", "delta"), ("lam", "lamb_params"), ("w2", "gate_w2"))},
        "rm_w1T": w["L0_attn_b_gate_w1"].T, "rm_nw": w["L0_attn_b_norm_weight"].reshape(2, P).T,
        "rm_wfb": np.concatenate([w["L0_attn_b_Wf"], w["L0_attn_b_Wbet"]], axis=1),
        **{"rm_" + n: v for n, v in ridge_constants(8, 1024).items()},
        "ident": np.eye(P, dtype=np.float32),
    }


def program(nc, a, layers="AFCFSTGT"):
    B, T, _ = a["x"].shape
    NT = B * T // P
    with ExitStack() as ctx:
        X = ctx.enter_context(nc.sbuf_tensor("X", [P, NT, D], F32))
        ident = ctx.enter_context(nc.sbuf_tensor("ident_sb", [P, P], F32))
        eps = ctx.enter_context(nc.sbuf_tensor("eps", [P, 2], F32))
        identb = ctx.enter_context(nc.sbuf_tensor("identb", [P, P], BF16))
        s_in = ctx.enter_context(nc.semaphore("x_in"))
        s_eps = ctx.enter_context(nc.semaphore("eps_set"))
        with nc.Block() as block:

            @block.sync
            def _(sp):
                sp.dma_start(X[:, :, :], a["x"].rearrange("b (t p) d -> p (b t) d", p=P)).then_inc(s_in, 16)
                sp.dma_start(ident[:, :], a["ident"]).then_inc(s_in, 16)
                sp.wait_ge(s_in, 32)

            @block.vector
            def _(dve):
                nc.vector.memset(eps[:, 0:1], 1e-5).then_inc(s_eps, 1)
                nc.vector.memset(eps[:, 1:2], 1e-6).then_inc(s_eps, 1)
                dve.wait_ge(s_in, 32)
                nc.vector.tensor_copy(identb[:, :], ident[:, :]).then_inc(s_eps, 1)

        for n, kind in enumerate(layers):
            name = f"l{n}"
            if kind == "T":
                linear3_tanh(nc, X, NT, name, {k: a["tr_" + k] for k in ("weightT", "aux1", "aux2", "bias")}, ident, eps)
            if kind == "F":
                token_ffn(nc, X, NT, name, {k[3:]: v for k, v in a.items() if k.startswith("ff_")}, ident, eps)
            if kind == "G":
                attention(nc, X, B, T, name, {k[3:]: v for k, v in a.items() if k.startswith("ga_")}, ident, identb, eps, False)
            if kind == "S":
                attention(nc, X, B, T, name, {k[3:]: v for k, v in a.items() if k.startswith("sa_")}, ident, identb, eps, True)
            if kind == "A":
                delta_rule(nc, X, B, T, name, {k[3:]: v for k, v in a.items() if k.startswith("dr_")}, ident, eps)
            if kind == "C":
                ridge_memory(nc, X, B, T, name, {k[3:]: v for k, v in a.items() if k.startswith("rm_")}, ident, identb, eps)
        with nc.Block() as block:

            @block.sync
            def _(sp):
                sp.dma_start(a["out"].rearrange("b (t p) d -> p (b t) d", p=P), X[:, :, :]).then_inc(s_in, 16)
                sp.wait_ge(s_in, 48)


def kernel(**inputs):
    import numpy as _np
    import concourse.bacc as _bacc
    from concourse import mybir as _mybir
    from concourse.bass_utils import run_bass_kernel_spmd as _run

    w = {name: _np.asarray(a) for name, a in inputs.items()}
    arrays = {name: _np.ascontiguousarray(a) for name, a in lay_out(w).items()}
    arrays["x"] = _np.ascontiguousarray(w["L0_attn_a_out"])
    nc = _bacc.Bacc("TRN2", target_bir_lowering=False, num_devices=1)
    aps = {name: nc.dram_tensor(name, a.shape, _mybir.dt.from_np(a.dtype), kind="ExternalInput").ap()
           for name, a in arrays.items()}
    aps["out"] = nc.dram_tensor("out", arrays["x"].shape, _mybir.dt.float32, kind="ExternalOutput").ap()
    program(nc, aps)
    r = _run(nc, [arrays], core_ids=[0])
    return r.results[0]["out"]
```
